# Optimizing a Trainium2 kernel written in Bass

```python
import numpy as np
import jax
import jax.numpy as jnp

def _softmax(x, axis=-1):
    return jax.nn.softmax(x, axis=axis)

def _gelu(x):
    return jax.nn.gelu(x, approximate=True)

def _silu(x):
    return jax.nn.silu(x)

def _sigmoid(x):
    return jax.nn.sigmoid(x)

def _layernorm(x, axis=-1, eps=1e-05):
    m = jnp.mean(x, axis=axis, keepdims=True)
    v = jnp.var(x, axis=axis, keepdims=True)
    return (x - m) / jnp.sqrt(v + eps)

def _scatter_add(tgt, idx, src, axis=0):
    return tgt.at[idx].add(src)

def _segment_sum(src, seg, n):
    return jax.ops.segment_sum(src, seg, n)
kernel_name = 'mk_seq_preln_d1_jaxref_r4_bfeaa9'

def setup_inputs(seed: int=0):
    np.random.seed(seed)
    _w = jnp.asarray

    def _L0_attn_setup():
        import jax, jax.numpy as jnp
        import numpy as np
        from jax import lax
        DIM = 256
        B, N = (4, 1024)

        def _rmsnorm(x, gamma):
            scale = jnp.asarray(x.shape[-1], x.dtype) ** 0.5
            norm = jnp.sqrt(jnp.sum(x * x, axis=-1, keepdims=True))
            return x / jnp.maximum(norm, 1e-12) * scale * gamma
        key = jax.random.key(seed)
        k1, k2 = jax.random.split(key)
        x = jax.random.normal(k1, (B, N, DIM), dtype=jnp.float32)
        w_qkva = jax.random.normal(k2, (3 * DIM, DIM), dtype=jnp.float32) * DIM ** (-0.5)
        gamma = jnp.ones((DIM,), dtype=jnp.float32)
        return {'x': x, 'w_qkva': w_qkva, 'gamma': gamma}
    _L0_attn_in = _L0_attn_setup()

    def _L0_ffn_setup():
        import jax, jax.numpy as jnp
        import numpy as np
        D_MODEL = 256
        HIDDEN = 1024
        NUM_ROUTED = 7
        TOP_K = 2

        def _swiglu(x_flat, wg, wu, wd):
            g = jnp.einsum('nd,edh->enh', x_flat, wg)
            u = jnp.einsum('nd,edh->enh', x_flat, wu)
            h = jax.nn.silu(g) * u
            return jnp.einsum('enh,ehd->end', h, wd)
        key = jax.random.key(seed)
        ks = jax.random.split(key, 8)
        s = 0.02
        return {'x': jax.random.normal(ks[0], (4, 512, D_MODEL), jnp.float32), 'router_w': jax.random.normal(ks[1], (NUM_ROUTED, D_MODEL), jnp.float32) * s, 'w_gate': jax.random.normal(ks[2], (NUM_ROUTED, D_MODEL, HIDDEN), jnp.float32) * s, 'w_up': jax.random.normal(ks[3], (NUM_ROUTED, D_MODEL, HIDDEN), jnp.float32) * s, 'w_down': jax.random.normal(ks[4], (NUM_ROUTED, HIDDEN, D_MODEL), jnp.float32) * s, 'sw_gate': jax.random.normal(ks[5], (1, D_MODEL, HIDDEN), jnp.float32) * s, 'sw_up': jax.random.normal(ks[6], (1, D_MODEL, HIDDEN), jnp.float32) * s, 'sw_down': jax.random.normal(ks[7], (1, HIDDEN, D_MODEL), jnp.float32) * s}
    _L0_ffn_in = _L0_ffn_setup()
    _d = {'L0_attn_x': _L0_attn_in['x'], 'L0_attn_w_qkva': _L0_attn_in['w_qkva'], 'L0_attn_gamma': _L0_attn_in['gamma'], 'L0_ffn_router_w': _L0_ffn_in['router_w'], 'L0_ffn_w_gate': _L0_ffn_in['w_gate'], 'L0_ffn_w_up': _L0_ffn_in['w_up'], 'L0_ffn_w_down': _L0_ffn_in['w_down'], 'L0_ffn_sw_gate': _L0_ffn_in['sw_gate'], 'L0_ffn_sw_up': _L0_ffn_in['sw_up'], 'L0_ffn_sw_down': _L0_ffn_in['sw_down']}
    _x0 = _d['L0_attn_x']
    _d['L0_attn_x'] = jax.random.normal(jax.random.fold_in(jax.random.key(seed), 1), (4, 1024, 256), dtype=_x0.dtype)
    del _x0
    return _d

def reference(L0_attn_x, L0_attn_w_qkva, L0_attn_gamma, L0_ffn_router_w, L0_ffn_w_gate, L0_ffn_w_up, L0_ffn_w_down, L0_ffn_sw_gate, L0_ffn_sw_up, L0_ffn_sw_down):

    def _L0_attn_ref(x, w_qkva, gamma):
        import jax, jax.numpy as jnp
        import numpy as np
        from jax import lax
        DIM = 256
        B, N = (4, 1024)

        def _rmsnorm(x, gamma):
            scale = jnp.asarray(x.shape[-1], x.dtype) ** 0.5
            norm = jnp.sqrt(jnp.sum(x * x, axis=-1, keepdims=True))
            return x / jnp.maximum(norm, 1e-12) * scale * gamma
        h = _rmsnorm(x, gamma)
        qkva = jnp.einsum('bnd,ed->bne', h, w_qkva)
        q, kv, a = jnp.split(qkva, 3, axis=-1)
        a = jax.nn.sigmoid(a)

        def binary_operator(e_i, e_j):
            a_i, kv_i = e_i
            a_j, kv_j = e_j
            return (a_j * a_i, a_j * kv_i + kv_j)
        _, y = lax.associative_scan(binary_operator, (a, kv), axis=1)
        return q * y

    def _L0_ffn_ref(x, router_w, w_gate, w_up, w_down, sw_gate, sw_up, sw_down):
        import jax, jax.numpy as jnp
        import numpy as np
        D_MODEL = 256
        HIDDEN = 1024
        NUM_ROUTED = 7
        TOP_K = 2

        def _swiglu(x_flat, wg, wu, wd):
            g = jnp.einsum('nd,edh->enh', x_flat, wg)
            u = jnp.einsum('nd,edh->enh', x_flat, wu)
            h = jax.nn.silu(g) * u
            return jnp.einsum('enh,ehd->end', h, wd)
        orig_shape = x.shape
        x_flat = x.reshape(-1, orig_shape[-1])
        N = x_flat.shape[0]
        logits = x_flat @ router_w.T
        top_vals, top_idx = jax.lax.top_k(logits, TOP_K)
        top_w = jax.nn.softmax(top_vals, axis=-1)
        combine = jnp.sum(jax.nn.one_hot(top_idx, NUM_ROUTED, dtype=x.dtype) * top_w[..., None], axis=1)
        routed_out = _swiglu(x_flat, w_gate, w_up, w_down)
        mixed = jnp.einsum('end,ne->nd', routed_out, combine)
        shared_out = _swiglu(x_flat, sw_gate, sw_up, sw_down)
        mixed = mixed + jnp.mean(shared_out, axis=0)
        return mixed.reshape(orig_shape)
    x = L0_attn_x
    x = x + _L0_attn_ref(_layernorm(x, axis=-1), L0_attn_w_qkva, L0_attn_gamma)
    x = x + _L0_ffn_ref(_layernorm(x, axis=-1), L0_ffn_router_w, L0_ffn_w_gate, L0_ffn_w_up, L0_ffn_w_down, L0_ffn_sw_gate, L0_ffn_sw_up, L0_ffn_sw_down)
    return x

_drawn_inputs = setup_inputs


def setup_inputs(seed=0):
    import zlib

    import numpy as np

    out = dict(_drawn_inputs(seed))
    spreads = {'L0_attn_gamma': (1.0, 0.2)}
    factors = {'L0_ffn_router_w': 4.691,
     'L0_ffn_w_gate': 3.991,
     'L0_ffn_w_up': 3.944,
     'L0_ffn_w_down': 3.948,
     'L0_ffn_sw_gate': 2.85,
     'L0_ffn_sw_up': 2.817,
     'L0_ffn_sw_down': 2.818}
    for name, (base, spread) in spreads.items():
        noise = np.random.default_rng([zlib.crc32(name.encode()), seed]).standard_normal(out[name].shape)
        drawn = base * np.exp(spread * noise) if base else spread * noise
        out[name] = jnp.asarray(drawn.astype(out[name].dtype))
    for name, factor in factors.items():
        out[name] = (out[name] * factor).astype(out[name].dtype)
    return out
```

```python
from contextlib import ExitStack

import concourse.bass as bass
from concourse import mybir

F32 = mybir.dt.float32
F32R = mybir.dt.float32r
I32 = mybir.dt.int32
ALU = mybir.AluOpType
ACT = mybir.ActivationFunctionType
AX_X = mybir.AxisListType.X

P = 128
SLOT = 256
EPS = 1e-5
TINY2 = 1e-24
LOWEST = -3.0e38


def preln_scan_moe_kernel(nc, x, w_qkva, gamma, router_w, w_gate, w_up, w_down,
                          sw_gate, sw_up, sw_down, out):
    B, S, D = x.shape
    E, _, H = w_gate.shape
    N = B * S
    TILES = N // P
    BT = S // P
    CH = 512
    CT = CH // P
    KD = D // P
    JH = H // P
    EP = 8
    TOP = 2
    ST = SLOT // P
    SHARED = N // SLOT
    SA = SHARED // 2
    SBN = SHARED - SA
    ROUTED = (TOP * N + E * (SLOT - 1)) // SLOT
    ROUTED += ROUTED % 2
    THR = N // SLOT
    ZEROS = 4
    PAIRS = JH // 2
    WPART = KD * H
    assert B == 4 and S == 2 * CH and KD == 2 and WPART == JH * D and SA % 2 == 0 and E < EP

    x_t = x.rearrange("b (k p) d -> p (b k) d", p=P)
    out_t = out.rearrange("b (k p) d -> p (b k) d", p=P)
    z_dram = nc.dram_tensor("z_rows", [N, D], F32).ap()
    sorted_dram = nc.dram_tensor("sorted_rows", [ROUTED * SLOT, D], F32).ap()
    y_dram = nc.dram_tensor("expert_rows", [ROUTED * SLOT, D], F32).ap()

    def rows_of(dram, slot):
        return dram.rearrange("(s t p) d -> s p t d", p=P, t=ST)[bass.ds(slot, 1)].rearrange(
            "a p t d -> p (a t) d")

    with ExitStack() as ctx:
        base = [(nc.sbuf_base + 31) // 32 * 32]

        def place(name, shape, dtype=F32, at=None):
            free = 4
            for n in shape[1:]:
                free *= n
            if at is None:
                at = base[0]
                base[0] += (free + 31) // 32 * 32
            return nc.alloc_sbuf_tensor_at(name, shape, dtype, offset=at), at

        def sb(name, shape, dtype=F32, at=None):
            return place(name, shape, dtype, at)[0]

        resid = sb("resid", [P, TILES, D])
        raw = sb("raw", [P, 3, WPART])
        w_hi, w_lo, w_at = [], [], []
        for b in range(2):
            t, at = place(f"w_hi{b}", [P, 3, WPART], F32R)
            w_hi.append(t)
            w_at.append(at)
            w_lo.append(sb(f"w_lo{b}", [P, 3, WPART], F32R))
        h_hi, h_at = place("h_hi", [P, JH, SLOT], F32R)
        h_lo = sb("h_lo", [P, JH, SLOT], F32R)
        xs_hi, xs_at = place("xs_hi", [P, 2, KD, SLOT], F32R)
        xs_lo = sb("xs_lo", [P, 2, KD, SLOT], F32R)
        x_rows, rows_at = place("x_rows", [P, 2, ST, D])
        y_rows = sb("y_rows", [P, 2, ST, D])
        silu = sb("silu", [P, 2, 2, SLOT])
        h32, h32_at = place("h32", [P, 2, 2, SLOT])

        z_all = sb("z_all", [P, TILES, D], at=w_at[1])
        h_rows = sb("h_rows", [P, 2, CT, D], at=w_at[1] + 4 * TILES * D)
        hT = sb("hT", [P, 2, KD, CH], at=w_at[1] + 4 * (TILES + BT) * D)
        a_sb = sb("a_sb", [P, 2, KD, CH], at=h_at)
        y_sb = sb("y_sb", [P, 2, KD, CH], at=h_at + 8 * KD * CH)
        oT = sb("oT", [P, 2, KD, CH], at=xs_at)
        w_nat = sb("w_nat", [P, 3 * KD, D], at=rows_at)
        wT = sb("wT", [P, KD, 3 * D], at=rows_at + 12 * KD * D)
        incl = sb("incl", [P, EP, TILES], at=h32_at)
        cmp = sb("cmp", [P, EP, THR], at=h32_at + 1024)
        owner_c = sb("owner_c", [1, ROUTED, E], at=h32_at + 2048)
        GR = 8
        got = sb("got", [P, GR, TOP, D], at=w_at[0])

        ident = sb("ident", [P, P])
        below = sb("below", [P, P])
        ones = sb("ones", [P, P])
        zeros = sb("zeros", [P, D])
        eps8 = sb("eps8", [P, BT])
        half8 = sb("half8", [P, BT])
        r_nat = sb("r_nat", [E, D])
        rT = sb("rT", [P, KD, EP])
        g_nat = sb("g_nat", [KD, P])
        gT = sb("gT", [P, KD])
        stats = sb("stats", [P, BT, 6])
        mv = sb("mv", [P, BT, 2])
        mv1 = sb("mv1", [P, TILES, 2])
        mv2 = sb("mv2", [P, TILES, 2])
        scale1 = sb("scale1", [P, TILES])
        scale2 = sb("scale2", [P, TILES])
        pa = sb("pa", [P, BT])
        pr = sb("pr", [P, BT])
        pt = sb("pt", [P, BT])
        pv = sb("pv", [P, BT])
        pc = sb("pc", [P, BT])
        iota_i = sb("iota_i", [P, 64], I32)
        iota_f = sb("iota_f", [P, 64])
        DESC, SLOTS, THRS = iota_f[:, 0:EP], iota_f[0:1, EP:EP + ROUTED], iota_f[:, 48:48 + THR]
        assert EP + ROUTED <= 48 and THR <= 16
        logits = sb("logits", [P, TILES, EP])
        first = sb("first", [P, TOP, TILES, EP])
        tmp = sb("tmp", [P, TILES, EP])
        count = sb("count", [P, EP, TILES])
        keep = sb("keep", [P, EP, TILES])
        top = sb("top", [P, TOP, TILES])
        col = sb("col", [P, TILES])
        gap = sb("gap", [P, TILES])
        mix = sb("mix", [P, TOP, TILES])
        n_slots = sb("n_slots", [P, EP])
        s_incl = sb("s_incl", [P, EP])
        s_base = sb("s_base", [P, EP])
        pos_f = sb("pos_f", [P, TILES])
        pos = sb("pos", [P, TOP, TILES], I32)
        owner_f = sb("owner_f", [1, ROUTED])
        owner = sb("owner", [1, ROUTED], I32)
        assert base[0] <= nc.sbuf_usable_end, base[0]

        ps = ctx.enter_context(nc.psum_tensor("ps", [P, 8, 512], F32))

        def sem(name):
            return ctx.enter_context(nc.semaphore(name))

        x_in = sem("x_in")
        small_in = sem("small_in")
        raw_in = [sem(f"raw_in{k}") for k in range(3)]
        consts = sem("consts")
        pool_step = sem("pool_step")
        pool_scaled = sem("pool_scaled")
        bare = sem("bare")
        dve_step = sem("dve_step")
        prep = sem("prep")
        prep_done = sem("prep_done")
        mv_ready = sem("mv_ready")
        mv_taken = sem("mv_taken")
        scaled = sem("scaled")
        h_rows_ready = sem("h_rows_ready")
        hT_psum = sem("hT_psum")
        hT_ready = sem("hT_ready")
        a_psum, kv_psum, q_psum = sem("a_psum"), sem("kv_psum"), sem("q_psum")
        a_ready = sem("a_ready")
        y_ready = sem("y_ready")
        oT_ready = sem("oT_ready")
        o_psum = sem("o_psum")
        res_ready = sem("res_ready")
        stat = sem("stat")
        z_ready = sem("z_ready")
        z_out = [sem("z_out0"), sem("z_out1")]
        lg_psum = sem("lg_psum")
        lg_ready = sem("lg_ready")
        zeros_made = sem("zeros_made")
        zero_in = sem("zero_in")
        hot = sem("hot")
        pre_psum = sem("pre_psum")
        gap_ready = sem("gap_ready")
        mix_ready = sem("mix_ready")
        routed = sem("routed")
        scat = sem("scat")
        x_ld = [sem("x_ld0"), sem("x_ld1")]
        xT_psum = sem("xT_psum")
        xhi_ready = sem("xhi_ready")
        x_split = sem("x_split")
        whi_ready = [sem(f"whi_ready{k}") for k in range(3)]
        wlo_ready = [sem(f"wlo_ready{k}") for k in range(3)]
        gu_psum = sem("gu_psum")
        silu_ready = sem("silu_ready")
        gated = sem("gated")
        hhi_ready = sem("hhi_ready")
        h_ready = sem("h_ready")
        down_psum = sem("down_psum")
        down_free = sem("down_free")
        y_out = [sem("y_out0"), sem("y_out1")]
        got_in = [sem(f"got_in{k}") for k in range(GR)]
        mixed = sem("mixed")
        outs = sem("outs")

        NB0 = SA + ROUTED

        block = ctx.enter_context(nc.Block())

        def raw_rows(gate, up, down):
            return (gate.rearrange("(k p) h -> p k h", p=P), up.rearrange("(k p) h -> p k h", p=P),
                    down.rearrange("(j p) d -> p j d", p=P))

        raw_v = [raw[:, 0, :].rearrange("p (k h) -> p k h", k=KD),
                 raw[:, 1, :].rearrange("p (k h) -> p k h", k=KD),
                 raw[:, 2, :].rearrange("p (j d) -> p j d", j=JH)]

        @block.sync
        def _(sp):
            sp.dma_start(resid[:, 0:BT, :], x_t[:, 0:BT, :]).then_inc(x_in, 16)
            with sp.Fori(1, B) as b:
                sp.wait_ge(x_in, b * 16)
                sp.dma_start(resid[:, bass.ds(b * BT, BT), :], x_t[:, bass.ds(b * BT, BT), :]
                             ).then_inc(x_in, 16)
            for k, src in enumerate(raw_rows(sw_gate[0], sw_up[0], sw_down[0])):
                sp.dma_start(raw_v[k], src).then_inc(raw_in[k], 16)

            z_v = z_dram.rearrange("(g k p) d -> g p k d", p=P, k=CT)
            with sp.Fori(0, B) as b:
                for c in range(2):
                    g = b * 2 + c
                    sp.wait_ge(z_ready, g + 1)
                    sp.dma_start(z_v[bass.ds(g, 1)].rearrange("a p k d -> p (a k) d"),
                                 h_rows[:, c, :, :]).then_inc(z_out[c], 16)
                    sp.dma_start(z_all[:, bass.ds(g * CT, CT), :], h_rows[:, c, :, :]
                                 ).then_inc(z_out[c], 16)

            def load_x(n, slot, dram, par, at):
                sp.wait_ge(xT_psum, n + 1)
                sp.dma_start(x_rows[:, par, :, :], rows_of(dram, slot)).then_inc(x_ld[par], 16)

            def load_w(sources, m):
                for k, src in enumerate(sources):
                    sp.wait_ge(wlo_ready[k], m)
                    sp.dma_start(raw_v[k], src).then_inc(raw_in[k], 16)

            def load_expert(r, m):
                e = sp.value_load(owner[0:1, bass.ds(r, 1)], min_val=0, max_val=E - 1)
                def of(w):
                    return w[bass.ds(e, 1)].rearrange("a r c -> (a r) c")
                load_w(raw_rows(of(w_gate), of(w_up), of(w_down)), m)

            sp.wait_ge(lg_psum, 2 * B + 1)
            for c in range(2):
                sp.wait_ge(z_out[c], 32 * (B + 1))
            load_x(0, 0, z_dram, 0, 0)
            load_x(1, 1, z_dram, 1, 0)
            sp.wait_ge(routed, 2)
            load_expert(0, 1)
            with sp.Fori(1, SA // 2) as i:
                for u in range(2):
                    load_x(i * 2 + u, i * 2 + u, z_dram, u, i)
            sp.wait_ge(scat, 16 * TOP * TILES)
            with sp.Fori(0, ROUTED // 2 - 1) as i:
                for u in range(2):
                    load_x(i * 2 + (SA + u), i * 2 + u, sorted_dram, u, i)
                    load_expert(i * 2 + (u + 1), i * 2 + (u + 2))
            load_x(NB0 - 2, ROUTED - 2, sorted_dram, 0, 0)
            load_expert(ROUTED - 1, ROUTED)
            load_x(NB0 - 1, ROUTED - 1, sorted_dram, 1, 0)
            load_w(raw_rows(sw_gate[0], sw_up[0], sw_down[0]), ROUTED + 1)
            for u in range(2):
                load_x(NB0 + u, SA + u, z_dram, u, 0)

            def store(i):
                sp.wait_ge(mixed, i * 2 * GR + 2 * GR)
                sp.wait_ge(down_free, i * 2 + (NB0 + 3))
                for half in range(2):
                    t0 = i * CT + half * (TILES // 2)
                    sp.dma_start(out_t[:, bass.ds(t0, CT), :], resid[:, bass.ds(t0, CT), :]
                                 ).then_inc(outs, 16)

            with sp.Fori(0, SBN // 2 - 1) as i:
                for u in range(2):
                    load_x(i * 2 + (NB0 + 2 + u), i * 2 + (SA + 2 + u), z_dram, u, i)
                store(i)
            store(SBN // 2 - 1)
            sp.wait_ge(outs, 16 * SBN)
            for u in range(2):
                sp.wait_ge(y_out[u], 16 + 16 * (ROUTED // 2))
            sp.wait_ge(zero_in, 16 * ZEROS)

        @block.gpsimd
        def _(pool):
            made = [0]

            def own(ins):
                made[0] += 1
                ins.then_inc(pool_step, 1)

            own(pool.memset(ident[:, :], 0.0))
            own(pool.memset(below[:, :], 1.0))
            own(pool.memset(ones[:, :], 1.0))
            own(pool.memset(eps8[:, :], EPS))
            own(pool.memset(half8[:, :], -0.5))
            own(pool.iota(iota_i[:, 0:EP], pattern=[[-1, EP]], base=EP, channel_multiplier=0))
            own(pool.iota(iota_i[:, EP:48], pattern=[[1, 48 - EP]], base=0, channel_multiplier=0))
            own(pool.iota(iota_i[:, 48:64], pattern=[[SLOT, 16]], base=0, channel_multiplier=0))
            pool.wait_ge(pool_step, made[0])
            pool.affine_select(out=ident[:, :], in_=ident[:, :], compare_op=ALU.not_equal, fill=1.0,
                               base=0, pattern=[[-1, P]], channel_multiplier=1).then_inc(consts, 1)
            pool.affine_select(out=below[:, :], in_=below[:, :], compare_op=ALU.is_gt, fill=0.0,
                               base=0, pattern=[[1, P]], channel_multiplier=-1).then_inc(consts, 1)
            pool.tensor_copy(iota_f[:, :], iota_i[:, :]).then_inc(consts, 1)

            STEPS1, STEPS2 = 16, 6

            def stepper(b, before, steps):
                done = [0]

                def step(ins):
                    done[0] += 1
                    assert done[0] <= steps
                    ins.then_inc(pool_step, 1)
                    pool.wait_ge(pool_step, b * steps + (before + done[0]))
                    pool.sem_inc(bare, 1)
                return step

            def inv_sqrt(step):
                step(pool.tensor_tensor(pr[:, :], pa[:, :], half8[:, :], ALU.pow))
                step(pool.tensor_tensor(pt[:, :], pr[:, :], pr[:, :], ALU.mult))
                step(pool.tensor_tensor(pt[:, :], pt[:, :], pa[:, :], ALU.mult))
                step(pool.tensor_scalar(pt[:, :], pt[:, :], -0.5, 1.5, ALU.mult, ALU.add))

            with pool.Fori(0, B) as b:
                step = stepper(b, made[0], STEPS1)
                tiles = bass.ds(b * BT, BT)
                pool.wait_ge(mv_ready, b + 1)
                pool.sem_inc(bare, 1)
                step(pool.tensor_copy(mv1[:, tiles, :], mv[:, :, :]))
                step(pool.tensor_copy(pv[:, :], mv[:, :, 1]))
                pool.sem_inc(mv_taken, 1)
                step(pool.tensor_tensor(pa[:, :], pv[:, :], eps8[:, :], ALU.add))
                inv_sqrt(step)
                step(pool.tensor_tensor(pc[:, :], pr[:, :], pt[:, :], ALU.mult))
                step(pool.tensor_tensor(pa[:, :], pc[:, :], pc[:, :], ALU.mult))
                step(pool.tensor_tensor(pa[:, :], pa[:, :], pv[:, :], ALU.mult))
                step(pool.tensor_scalar(pa[:, :], pa[:, :], float(D), TINY2, ALU.mult, ALU.max))
                inv_sqrt(step)
                step(pool.tensor_tensor(pt[:, :], pt[:, :], pr[:, :], ALU.mult))
                pool.tensor_scalar(pc[:, :], pc[:, :], float(D) ** 0.5, None, ALU.mult
                                   ).then_inc(pool_scaled, 1)
                pool.wait_ge(pool_scaled, b + 1)
                pool.tensor_tensor(scale1[:, tiles], pc[:, :], pt[:, :], ALU.mult).then_inc(scaled, 1)
            before = made[0] + B * STEPS1

            with pool.Fori(0, B) as b:
                step = stepper(b, before, STEPS2)
                tiles = bass.ds(b * BT, BT)
                pool.wait_ge(mv_ready, b + (B + 1))
                pool.sem_inc(bare, 1)
                step(pool.tensor_copy(mv2[:, tiles, :], mv[:, :, :]))
                step(pool.tensor_tensor(pa[:, :], mv[:, :, 1], eps8[:, :], ALU.add))
                pool.sem_inc(mv_taken, 1)
                inv_sqrt(step)
                pool.tensor_tensor(scale2[:, tiles], pr[:, :], pt[:, :], ALU.mult).then_inc(scaled, 1)
                pool.wait_ge(scaled, b + (B + 1))

            def split_lo(m, buf):
                for k in range(3):
                    pool.wait_ge(whi_ready[k], m + 1)
                    pool.tensor_tensor(w_lo[buf][:, k, :], raw[:, k, :], w_hi[buf][:, k, :].bitcast(F32),
                                       ALU.subtract).then_inc(wlo_ready[k], 1)

            split_lo(0, 0)
            for c in range(2):
                pool.wait_ge(z_out[c], 32 * (B + 1))
            pool.wait_ge(zero_in, ZEROS * 16)
            pool.wait_ge(routed, 2)
            for t in range(TILES):
                for k in range(TOP):
                    pool.indirect_dma_start(
                        sorted_dram, bass.IndirectOffsetOnAxis(ap=pos[:, k, t:t + 1], axis=0),
                        z_all[:, t, :], None, bounds_check=ROUTED * SLOT - 1).then_inc(scat, 16)
            split_lo(1, 1)
            with pool.Fori(0, ROUTED // 2) as i:
                for u in range(2):
                    split_lo(i * 2 + (u + 2), u)

            for u in range(2):
                pool.wait_ge(y_out[u], 16 + 16 * (ROUTED // 2))
            for i in range(TILES // GR):
                for r in range(GR):
                    t = i * CT + r % CT + (r // CT) * (TILES // 2)
                    if i:
                        pool.wait_ge(mixed, TOP * ((i - 1) * GR + r + 1))
                    for k in range(TOP):
                        pool.indirect_dma_start(
                            got[:, r, k, :], None, y_dram,
                            bass.IndirectOffsetOnAxis(ap=pos[:, k, t:t + 1], axis=0),
                            bounds_check=ROUTED * SLOT - 1).then_inc(got_in[r], 16)

        @block.scalar
        def _(act):
            for k, (dst, src) in enumerate((
                    (w_nat[:, :, :], w_qkva.rearrange("(e p) d -> p e d", p=P)),
                    (g_nat[:, :], gamma.rearrange("(k p) -> k p", p=P)),
                    (r_nat[:, :], router_w))):
                act.dma_start(dst, src).then_inc(small_in, 16)
            act.wait_ge(zeros_made, 1)
            rows = sorted_dram.rearrange("(z k p) d -> z p k d", p=P, z=ZEROS)
            for z in range(ZEROS):
                act.dma_start(rows[z], zeros[:, :].unsqueeze(1).broadcast_to([P, rows.shape[2], D])
                              ).then_inc(zero_in, 16)

            act.wait_ge(prep, 1)
            act.activation(gT[:, :], ps[:, 6, 0:KD], ACT.Copy).then_inc(prep_done, 1)
            act.activation(rT[:, :, 0:E], ps[:, 7, 0:KD * E].rearrange("p (k e) -> p k e", k=KD),
                           ACT.Copy).then_inc(prep_done, 1)
            act.wait_ge(prep_done, 1)
            for k in range(KD):
                act.activation(wT[:, k, :].rearrange("p (a n) -> p a n", a=2),
                               ps[:, 2 * k:2 * k + 2, 0:3 * P], ACT.Copy,
                               scale=gT[:, k:k + 1]).then_inc(prep_done, 1)

            with act.Fori(0, B) as b:
                for c in range(2):
                    g = b * 2 + c
                    act.wait_ge(hT_psum, g + 2)
                    act.wait_ge(q_psum, g + 1)
                    act.activation(hT[:, c, :, :], ps[:, 0:2, :], ACT.Copy).then_inc(hT_ready, 1)
                for c in range(2):
                    g = b * 2 + c
                    act.wait_ge(a_psum, g + 1)
                    act.wait_ge(y_ready, g * 2 + 2)
                    at = 2 + 2 * c
                    act.activation(a_sb[:, c, :, :], ps[:, at:at + 2, :], ACT.Sigmoid
                                   ).then_inc(a_ready, 1)
            with act.Fori(0, B) as b:
                for c in range(2):
                    g = b * 2 + c
                    act.wait_ge(hT_psum, g + (2 * B + 2))
                    if c == 0:
                        act.wait_ge(lg_psum, b * 2 + 1)
                    act.activation(hT[:, c, :, :], ps[:, 2 * c:2 * c + 2, :], ACT.Copy
                                   ).then_inc(hT_ready, 1)
            act.wait_ge(gap_ready, 1)
            act.activation(mix[:, 0, :], gap[:, :], ACT.Sigmoid).then_inc(mix_ready, 1)
            act.activation(mix[:, 1, :], gap[:, :], ACT.Sigmoid, scale=-1.0).then_inc(mix_ready, 1)

            def x_hi(n, par):
                act.wait_ge(xT_psum, n + 3)
                act.activation(xs_hi[:, par, :, :], ps[:, 6, :].rearrange("p (k n) -> p k n", k=KD),
                               ACT.Copy).then_inc(xhi_ready, 1)

            def slot(n, u, r=None, last=False):
                for p in range(PAIRS):
                    q = n * PAIRS + p
                    par = p % 2
                    act.wait_ge(gu_psum, q + 1)
                    act.activation(silu[:, par, :, :], ps[:, 2 * par:2 * par + 2, 0:SLOT], ACT.Silu
                                   ).then_inc(silu_ready, 1)
                    act.wait_ge(gated, q + 3)
                    if p == 0:
                        act.wait_ge(down_psum, n + 1)
                    act.activation(h_hi[:, 2 * p:2 * p + 2, :], h32[:, par, :, :], ACT.Copy
                                   ).then_inc(hhi_ready, 1)
                if not last:
                    x_hi(n + 1, 1 - u)
                if r is not None:
                    act.wait_ge(down_psum, n + 2)
                    act.wait_ge(y_out[u], r)
                    act.activation(y_rows[:, u, :, :], ps[:, 4:6, 0:D], ACT.Copy
                                   ).then_inc(down_free, 1)
                    act.wait_ge(down_free, n + 2)
                    act.dma_start(rows_of(y_dram, n - SA), y_rows[:, u, :, :]).then_inc(y_out[u], 16)

            x_hi(0, 0)
            with act.Fori(0, SA // 2) as i:
                for u in range(2):
                    slot(i * 2 + u, u)
            with act.Fori(0, ROUTED // 2) as i:
                for u in range(2):
                    slot(i * 2 + (SA + u), u, r=i * 16 + 16)
            with act.Fori(0, SBN // 2 - 1) as i:
                for u in range(2):
                    slot(i * 2 + (NB0 + u), u)
            slot(NB0 + SBN - 2, 0)
            slot(NB0 + SBN - 1, 1, last=True)

        @block.tensor
        def _(pe):
            pe.wait_ge(consts, 3)
            pe.wait_ge(small_in, 48)
            pe.transpose(ps[:, 6, 0:KD], g_nat[:, :], ident[0:KD, 0:KD])
            for k in range(KD):
                pe.transpose(ps[:, 7, k * E:k * E + E], r_nat[:, k * P:(k + 1) * P], ident[0:E, 0:E])
            for k in range(KD):
                for e in range(3 * KD):
                    last = pe.transpose(ps[:, 2 * k + e // 3, (e % 3) * P:(e % 3 + 1) * P],
                                        w_nat[:, e, k * P:(k + 1) * P], ident[:, :])
            last.then_inc(prep, 1)
            pe.wait_ge(prep_done, 2 + KD)

            def turn(c, bank):
                for kd in range(KD):
                    for k in range(CT):
                        last = pe.transpose(ps[:, bank + kd, k * P:(k + 1) * P],
                                            h_rows[:, c, k, kd * P:(kd + 1) * P], ident[:, :])
                last.then_inc(hT_psum, 1)

            def project(c, part, bank, signal):
                for e in range(KD):
                    for kd in range(KD):
                        at = (part * KD + e) * P
                        last = pe.matmul(ps[:, bank + e, :], wT[:, kd, at:at + P], hT[:, c, kd, :],
                                         start=kd == 0, stop=kd == KD - 1)
                last.then_inc(signal, 1)

            with pe.Fori(0, B) as b:
                for c in range(2):
                    g = b * 2 + c
                    pe.wait_ge(h_rows_ready, g + 1)
                    pe.wait_ge(hT_ready, g + 1)
                    turn(c, 0)
                for c in range(2):
                    g = b * 2 + c
                    pe.wait_ge(hT_ready, g + 2)
                    one, two = 2 + 2 * c, 4 - 2 * c
                    pe.wait_ge(y_ready, g * 2 + 4)
                    project(c, 2, one, a_psum)
                    pe.wait_ge(oT_ready, g + 1)
                    project(c, 1, two, kv_psum)
                    pe.wait_ge(a_ready, g + 1)
                    project(c, 0, one, q_psum)
                for c in range(2):
                    g = b * 2 + c
                    pe.wait_ge(oT_ready, g + 2)
                    pe.wait_ge(res_ready, g + 1)
                    for k in range(CT):
                        for e in range(KD):
                            at = (k % 2) * D + e * P
                            last = pe.transpose(ps[:, 6 + k // 2, at:at + P],
                                                oT[:, c, e, k * P:(k + 1) * P], ident[:, :])
                    last.then_inc(o_psum, 1)

            with pe.Fori(0, B) as b:
                for c in range(2):
                    pe.wait_ge(z_ready, b * 2 + (c + 1))
                    turn(c, 2 * c)
                for c in range(2):
                    g = b * 2 + c
                    pe.wait_ge(hT_ready, g + (2 * B + 2))
                    pe.wait_ge(lg_ready, g + 1)
                    for k in range(CT):
                        for kd in range(KD):
                            last = pe.matmul(ps[:, 4 + c, k * EP:k * EP + E],
                                             hT[:, c, kd, k * P:(k + 1) * P], rT[:, kd, 0:E],
                                             start=kd == 0, stop=kd == KD - 1)
                    last.then_inc(lg_psum, 1)

            pe.wait_ge(hot, 1)
            flat = tmp[:, :, :].rearrange("p t e -> p (t e)")
            pe.matmul(ps[:, 7, 0:TILES * EP], below[:, :], flat, start=True, stop=True)
            pe.matmul(ps[:, 7, TILES * EP:2 * TILES * EP], ones[:, :], flat, start=True, stop=True
                      ).then_inc(pre_psum, 1)

            def turn_x(n, u, nth):
                pe.wait_ge(x_ld[u], nth)
                for t in range(ST):
                    for kd in range(KD):
                        last = pe.transpose(ps[:, 6, kd * SLOT + t * P:kd * SLOT + (t + 1) * P],
                                            x_rows[:, u, t, kd * P:(kd + 1) * P], ident[:, :])
                last.then_inc(xT_psum, 1)

            def slot(n, u, buf, nth, m=None, last_slot=False):
                pe.wait_ge(x_split, n + 1)
                if m is not None:
                    for k in range(2):
                        pe.wait_ge(wlo_ready[k], m + 1)
                hi, lo = w_hi[buf], w_lo[buf]
                for p in range(PAIRS):
                    q = n * PAIRS + p
                    pe.wait_ge(gated, q + 1)
                    for j in (2 * p, 2 * p + 1):
                        for part in range(2):
                            o = ps[:, 2 * (p % 2) + j % 2, part * SLOT:(part + 1) * SLOT]
                            at = [kd * H + j * P for kd in range(KD)]
                            terms = [(w, xx, kd) for kd in range(KD)
                                     for w, xx in ((hi, xs_hi), (hi, xs_lo), (lo, xs_hi))]
                            for i, (w, xx, kd) in enumerate(terms):
                                last = pe.matmul(o, w[:, part, at[kd]:at[kd] + P], xx[:, u, kd, :],
                                                 start=i == 0, stop=i == len(terms) - 1)
                    last.then_inc(gu_psum, 1)
                if not last_slot:
                    turn_x(n + 1, 1 - u, nth)
                if m is not None:
                    pe.wait_ge(wlo_ready[2], m + 1)
                pe.wait_ge(down_free, n + 1)
                for p in range(PAIRS):
                    pe.wait_ge(h_ready, n * PAIRS + (p + 3))
                    for j in (2 * p, 2 * p + 1):
                        for t in range(ST):
                            terms = ((h_hi, hi), (h_hi, lo), (h_lo, hi))
                            for i, (hh, w) in enumerate(terms):
                                last = pe.matmul(ps[:, 4 + t, 0:D], hh[:, j, t * P:(t + 1) * P],
                                                 w[:, 2, j * D:(j + 1) * D],
                                                 start=j == 0 and i == 0,
                                                 stop=j == JH - 1 and i == len(terms) - 1)
                last.then_inc(down_psum, 1)

            turn_x(0, 0, 16)
            for k in range(3):
                pe.wait_ge(wlo_ready[k], 1)
            with pe.Fori(0, SA // 2) as i:
                slot(i * 2, 0, 0, i * 16 + 16)
                slot(i * 2 + 1, 1, 0, i * 16 + 32)
            R0 = SA // 2
            with pe.Fori(0, ROUTED // 2) as i:
                slot(i * 2 + SA, 0, 1, i * 16 + 16 * (R0 + 1), m=i * 2 + 1)
                slot(i * 2 + (SA + 1), 1, 0, i * 16 + 16 * (R0 + 2), m=i * 2 + 2)
            B0 = NB0 // 2
            for k in range(3):
                pe.wait_ge(wlo_ready[k], ROUTED + 2)
            with pe.Fori(0, SBN // 2 - 1) as i:
                slot(i * 2 + NB0, 0, 1, i * 16 + 16 * (B0 + 1))
                slot(i * 2 + (NB0 + 1), 1, 1, i * 16 + 16 * (B0 + 2))
            slot(NB0 + SBN - 2, 0, 1, 16 * (B0 + SBN // 2))
            slot(NB0 + SBN - 1, 1, 1, None, last_slot=True)

        @block.vector
        def _(dve):
            for s, n in ((mv_taken, 1), (hT_psum, 1), (hT_ready, 1), (q_psum, 2), (y_ready, 4),
                         (oT_ready, 1), (o_psum, 2), (res_ready, 1), (lg_psum, 1), (lg_ready, 2),
                         (z_out[0], 32), (z_out[1], 32), (xT_psum, 2), (gated, 2), (h_ready, 2),
                         (down_psum, 1), (down_free, 1), (y_out[0], 16), (y_out[1], 16)):
                dve.sem_inc(s, n)
            made = [0]

            def step(ins):
                made[0] += 1
                ins.then_inc(dve_step, 1)
                dve.wait_ge(dve_step, made[0])

            dve.memset(zeros[:, :], 0.0).then_inc(zeros_made, 1)
            dve.memset(logits[:, :, E:EP], LOWEST)
            dve.memset(keep[:, :, 1:TILES], 1.0)
            step(dve.memset(keep[:, :, 0:1], 0.0))

            with dve.Fori(0, B) as b:
                dve.wait_ge(x_in, b * 16 + 16)
                dve.sem_inc(bare, 1)
                for k in range(BT):
                    last = dve.bn_stats(stats[:, k, :], resid[:, bass.ds(b * BT + k, 1), :]
                                        .rearrange("p a d -> p (a d)"))
                last.then_inc(stat, 1)
                dve.wait_ge(stat, b + 1)
                dve.wait_ge(mv_taken, b + 1)
                dve.sem_inc(bare, 1)
                for k in range(BT):
                    last = dve.bn_aggr(mv[:, k, :], stats[:, k, :])
                last.then_inc(mv_ready, 1)
                dve.wait_ge(mv_ready, b + 1)

            with dve.Fori(0, B) as b:
                dve.wait_ge(scaled, b + 1)
                dve.wait_ge(hT_psum, b * 2 + 1)
                for c in range(2):
                    for k in range(CT):
                        t = b * BT + (c * CT + k)
                        last = dve.tensor_scalar(h_rows[:, c, k:k + 1, :], resid[:, bass.ds(t, 1), :],
                                                 mv1[:, bass.ds(t, 1), 0], scale1[:, bass.ds(t, 1)],
                                                 ALU.subtract, ALU.mult)
                    last.then_inc(h_rows_ready, 1)
                for c in range(2):
                    g = b * 2 + c
                    kv, q = 4 - 2 * c, 2 + 2 * c
                    dve.wait_ge(a_ready, g + 1)
                    dve.wait_ge(kv_psum, g + 1)
                    for e in range(KD):
                        if c == 1:
                            dve.wait_ge(y_ready, g * 2 + (e + 3))
                        dve.tensor_tensor_scan(y_sb[:, c, e, :], a_sb[:, c, e, :], ps[:, kv + e, :],
                                               y_sb[:, 0, e, CH - 1:CH] if c else 0.0,
                                               ALU.mult, ALU.add).then_inc(y_ready, 1)
                    dve.wait_ge(q_psum, g + 3)
                    dve.wait_ge(y_ready, g * 2 + 6)
                    dve.wait_ge(o_psum, g + 1)
                    dve.tensor_tensor(oT[:, c, :, :], ps[:, q:q + 2, :], y_sb[:, c, :, :], ALU.mult
                                      ).then_inc(oT_ready, 1)
                for c in range(2):
                    g = b * 2 + c
                    t = b * BT + c * CT
                    dve.wait_ge(o_psum, g + 3)
                    dve.tensor_tensor(resid[:, bass.ds(t, CT), :],
                                      ps[:, 6:8, :].rearrange("p b (k d) -> p (b k) d", d=D),
                                      resid[:, bass.ds(t, CT), :], ALU.add).then_inc(res_ready, 1)
                    dve.wait_ge(res_ready, g + 2)
                    dve.sem_inc(bare, 1)
                    for k in range(CT):
                        last = dve.bn_stats(stats[:, c * CT + k, :], resid[:, bass.ds(t + k, 1), :]
                                            .rearrange("p a d -> p (a d)"))
                    last.then_inc(stat, 1)
                dve.wait_ge(stat, b * 2 + (B + 2))
                dve.wait_ge(mv_taken, b + (B + 1))
                dve.sem_inc(bare, 1)
                for k in range(BT):
                    last = dve.bn_aggr(mv[:, k, :], stats[:, k, :])
                last.then_inc(mv_ready, 1)
                dve.wait_ge(mv_ready, b + (B + 1))

            def split_hi(k, m, buf, load):
                dve.wait_ge(raw_in[k], load)
                dve.tensor_copy(w_hi[buf][:, k, :], raw[:, k, :]).then_inc(whi_ready[k], 1)

            for k in range(3):
                split_hi(k, 0, 0, 16)

            with dve.Fori(0, B) as b:
                dve.wait_ge(scaled, b + (B + 1))
                for c in range(2):
                    g = b * 2 + c
                    dve.wait_ge(z_out[c], b * 32 + 32)
                    dve.wait_ge(hT_psum, g + 2 * B)
                    for k in range(CT):
                        t = b * BT + (c * CT + k)
                        last = dve.tensor_scalar(h_rows[:, c, k:k + 1, :], resid[:, bass.ds(t, 1), :],
                                                 mv2[:, bass.ds(t, 1), 0], scale2[:, bass.ds(t, 1)],
                                                 ALU.subtract, ALU.mult)
                    last.then_inc(z_ready, 1)
                for c in range(2):
                    g = b * 2 + c
                    dve.wait_ge(lg_psum, g + 2)
                    dve.tensor_copy(logits[:, bass.ds(g * CT, CT), 0:E],
                                    ps[:, 4 + c, 0:CT * EP].rearrange("p (k e) -> p k e", e=EP)[:, :, 0:E]
                                    ).then_inc(lg_ready, 1)

            def over_experts(a):
                return a.unsqueeze(2).broadcast_to([P, TILES, EP])

            desc = DESC.unsqueeze(1).broadcast_to([P, TILES, EP])
            dve.wait_ge(lg_ready, 2 * B + 2)
            dve.wait_ge(consts, 3)
            for k in range(TOP):
                step(dve.tensor_reduce(top[:, k, :], logits[:, :, :], AX_X, ALU.max))
                step(dve.tensor_tensor(tmp[:, :, :], logits[:, :, :], over_experts(top[:, k, :]),
                                       ALU.is_equal))
                step(dve.tensor_tensor(tmp[:, :, :], tmp[:, :, :], desc, ALU.mult))
                step(dve.tensor_reduce(col[:, :], tmp[:, :, :], AX_X, ALU.max))
                step(dve.tensor_tensor(first[:, k, :, :], over_experts(col[:, :]), desc, ALU.is_equal))
                if k == 0:
                    step(dve.scalar_tensor_tensor(out=logits[:, :, :], in0=first[:, 0, :, :],
                                                  scalar=LOWEST, in1=logits[:, :, :],
                                                  op0=ALU.mult, op1=ALU.add))
            dve.tensor_tensor(gap[:, :], top[:, 0, :], top[:, 1, :], ALU.subtract).then_inc(gap_ready, 1)
            dve.tensor_tensor(tmp[:, :, :], first[:, 0, :, :], first[:, 1, :, :], ALU.add
                              ).then_inc(hot, 1)

            dve.wait_ge(pre_psum, 1)
            before = ps[:, 7, 0:TILES * EP].rearrange("p (t e) -> p t e", e=EP)
            total = ps[:, 7, TILES * EP:2 * TILES * EP].rearrange("p (t e) -> p e t", e=EP)
            step(dve.tensor_copy(count[:, :, :], total))
            step(dve.tensor_tensor_scan(incl[:, :, :].rearrange("p e t -> p (e t)"),
                                        keep[:, :, :].rearrange("p e t -> p (e t)"),
                                        count[:, :, :].rearrange("p e t -> p (e t)"),
                                        0.0, ALU.mult, ALU.add))
            step(dve.tensor_tensor(cmp[:, :, :], incl[:, :, TILES - 1:TILES].broadcast_to([P, EP, THR]),
                                   THRS.unsqueeze(1).broadcast_to([P, EP, THR]), ALU.is_gt))
            step(dve.tensor_reduce(n_slots[:, :], cmp[:, :, :], AX_X, ALU.add))
            step(dve.tensor_tensor_scan(s_incl[:, :], ones[:, 0:EP], n_slots[:, :], 0.0,
                                        ALU.mult, ALU.add))
            step(dve.tensor_tensor(s_base[:, :], s_incl[:, :], n_slots[:, :], ALU.subtract))
            step(dve.tensor_scalar(s_base[:, :], s_base[:, :], float(SLOT), None, ALU.mult))
            step(dve.tensor_tensor(count[:, :, :], incl[:, :, :], count[:, :, :], ALU.subtract))
            step(dve.tensor_tensor(count[:, :, :], count[:, :, :],
                                   s_base[:, :].unsqueeze(2).broadcast_to([P, EP, TILES]), ALU.add))
            step(dve.tensor_tensor(tmp[:, :, :], before, count[:, :, :].rearrange("p e t -> p t e"),
                                   ALU.add))
            for k in range(TOP):
                step(dve.tensor_tensor(first[:, k, :, :], first[:, k, :, :], tmp[:, :, :], ALU.mult))
                step(dve.tensor_reduce(pos_f[:, :], first[:, k, :, :], AX_X, ALU.add))
                ins = dve.tensor_copy(pos[:, k, :], pos_f[:, :])
                if k < TOP - 1:
                    step(ins)
            ins.then_inc(routed, 1)
            dve.tensor_tensor(owner_c[:, :, :], s_incl[0:1, 0:E].unsqueeze(1).broadcast_to([1, ROUTED, E]),
                              SLOTS.unsqueeze(2).broadcast_to([1, ROUTED, E]), ALU.is_le
                              ).then_inc(dve_step, 1)
            made[0] += 1
            dve.wait_ge(dve_step, made[0])
            step(dve.tensor_reduce(owner_f[:, :], owner_c[:, :, :], AX_X, ALU.add))
            step(dve.tensor_scalar(owner_f[:, :], owner_f[:, :], float(E - 1), None, ALU.min))
            dve.tensor_copy(owner[:, :], owner_f[:, :]).then_inc(routed, 1)

            def x_lo(n, par):
                dve.wait_ge(xhi_ready, n + 1)
                dve.tensor_tensor(xs_lo[:, par, :, :], ps[:, 6, :].rearrange("p (k n) -> p k n", k=KD),
                                  xs_hi[:, par, :, :].bitcast(F32), ALU.subtract).then_inc(x_split, 1)

            def mix_tile(r, k, t, n_mixed, n_got):
                if k == 0:
                    dve.wait_ge(got_in[r], n_got)
                else:
                    dve.wait_ge(mixed, n_mixed)
                row = resid[:, bass.ds(t, 1), :]
                dve.scalar_tensor_tensor(out=row, in0=got[:, r, k:k + 1, :],
                                         scalar=mix[:, k, bass.ds(t, 1)], in1=row,
                                         op0=ALU.mult, op1=ALU.add).then_inc(mixed, 1)

            def slot(n, u, m=None, load=None, shared=None, back=None, last=False):
                for p in range(PAIRS):
                    q = n * PAIRS + p
                    par = p % 2
                    dve.wait_ge(silu_ready, q + 1)
                    dve.wait_ge(h_ready, q + 1)
                    dve.tensor_tensor(h32[:, par, :, :], ps[:, 2 * par:2 * par + 2, SLOT:2 * SLOT],
                                      silu[:, par, :, :], ALU.mult).then_inc(gated, 1)
                    if m is not None and p < 3:
                        if p < 2:
                            dve.wait_ge(gu_psum, n * PAIRS)
                        else:
                            dve.wait_ge(down_psum, n + 1)
                        split_hi(p, m, u, load)
                    if back is not None:
                        r = u * CT + p
                        t = back * CT + (p + u * (TILES // 2))
                        done = back * (TOP * GR) + (TOP * r + 1)
                        mix_tile(r, 0, t, None, back * (16 * TOP) + 16 * TOP)
                    dve.wait_ge(hhi_ready, q + 1)
                    dve.tensor_tensor(h_lo[:, 2 * p:2 * p + 2, :], h32[:, par, :, :],
                                      h_hi[:, 2 * p:2 * p + 2, :].bitcast(F32), ALU.subtract
                                      ).then_inc(h_ready, 1)
                    if back is not None:
                        mix_tile(r, 1, t, done, None)
                if not last:
                    x_lo(n + 1, 1 - u)
                if shared is not None:
                    dve.wait_ge(down_psum, n + 2)
                    if back is not None:
                        dve.wait_ge(mixed, back * (TOP * GR) + TOP * CT * (u + 1))
                    rows = resid[:, bass.ds(shared, ST), :]
                    dve.tensor_tensor(rows, ps[:, 4:6, 0:D], rows, ALU.add).then_inc(down_free, 1)
                    dve.wait_ge(down_free, n + 2)

            x_lo(0, 0)
            with dve.Fori(0, SA // 2) as i:
                for u in range(2):
                    slot(i * 2 + u, u, shared=i * (2 * ST) + u * ST)
            dve.wait_ge(scat, 16 * TOP * TILES)
            for k in range(3):
                split_hi(k, 1, 1, 32)
            with dve.Fori(0, ROUTED // 2) as i:
                for u in range(2):
                    slot(i * 2 + (SA + u), u, m=i * 2 + (2 + u), load=i * 32 + (48 + 16 * u))
            dve.wait_ge(mix_ready, TOP)
            with dve.Fori(0, SBN // 2 - 1) as i:
                for u in range(2):
                    slot(i * 2 + (NB0 + u), u, shared=i * (2 * ST) + (TILES // 2 + u * ST), back=i)
            i = SBN // 2 - 1
            for u in range(2):
                slot(i * 2 + NB0 + u, u, shared=i * 2 * ST + TILES // 2 + u * ST, back=i, last=u == 1)


_INS = ['L0_attn_x', 'L0_attn_w_qkva', 'L0_attn_gamma', 'L0_ffn_router_w', 'L0_ffn_w_gate',
        'L0_ffn_w_up', 'L0_ffn_w_down', 'L0_ffn_sw_gate', 'L0_ffn_sw_up', 'L0_ffn_sw_down']


def kernel(**inputs):
    import numpy as _np
    import concourse.bacc as _bacc
    from concourse import mybir as _mybir
    from concourse.bass_utils import run_bass_kernel_spmd as _run

    nc = _bacc.Bacc("TRN2", target_bir_lowering=False, num_devices=1)
    arrays, args = {}, []
    for name in _INS:
        a = _np.ascontiguousarray(inputs[name])
        arrays[f"in_{name}_dram"] = a
        args.append(nc.dram_tensor(f"in_{name}_dram", a.shape, _mybir.dt.from_np(a.dtype), kind="ExternalInput").ap())
    shape = inputs['L0_attn_x'].shape
    args.append(nc.dram_tensor("out_0_dram", shape, _mybir.dt.float32, kind="ExternalOutput").ap())
    preln_scan_moe_kernel(nc, *args)
    r = _run(nc, [arrays], core_ids=[0])
    return r.results[0]["out_0_dram"]
```

```python
from contextlib import ExitStack

import concourse.bass as bass
from concourse import mybir

F32 = mybir.dt.float32
F32R = mybir.dt.float32r
I32 = mybir.dt.int32
ALU = mybir.AluOpType
ACT = mybir.ActivationFunctionType
AX_X = mybir.AxisListType.X

P = 128
SLOT = 256
EPS = 1e-5
TINY2 = 1e-24
LOWEST = -3.0e38


def preln_scan_moe_kernel(nc, x, w_qkva, gamma, router_w, w_gate, w_up, w_down,
                          sw_gate, sw_up, sw_down, out):
    B, S, D = x.shape
    E, _, H = w_gate.shape
    N = B * S
    TILES = N // P
    BT = S // P
    CH = 512
    CT = CH // P
    KD = D // P
    JH = H // P
    EP = 8
    TOP = 2
    ST = SLOT // P
    SHARED = N // SLOT
    SA = SHARED // 2
    SBN = SHARED - SA
    ROUTED = (TOP * N + E * (SLOT - 1)) // SLOT
    ROUTED += ROUTED % 2
    THR = N // SLOT
    ZEROS = 4
    PAIRS = JH // 2
    WPART = KD * H
    assert B == 4 and S == 2 * CH and KD == 2 and WPART == JH * D and SA % 2 == 0 and E < EP

    x_t = x.rearrange("b (k p) d -> p (b k) d", p=P)
    out_t = out.rearrange("b (k p) d -> p (b k) d", p=P)
    z_dram = nc.dram_tensor("z_rows", [N, D], F32).ap()
    sorted_dram = nc.dram_tensor("sorted_rows", [ROUTED * SLOT, D], F32).ap()
    y_dram = nc.dram_tensor("expert_rows", [ROUTED * SLOT, D], F32).ap()

    def rows_of(dram, slot):
        return dram.rearrange("(s t p) d -> s p t d", p=P, t=ST)[bass.ds(slot, 1)].rearrange(
            "a p t d -> p (a t) d")

    with ExitStack() as ctx:
        base = [(nc.sbuf_base + 31) // 32 * 32]

        def place(name, shape, dtype=F32, at=None):
            free = 4
            for n in shape[1:]:
                free *= n
            if at is None:
                at = base[0]
                base[0] += (free + 31) // 32 * 32
            return nc.alloc_sbuf_tensor_at(name, shape, dtype, offset=at), at

        def sb(name, shape, dtype=F32, at=None):
            return place(name, shape, dtype, at)[0]

        resid = sb("resid", [P, TILES, D])
        raw = sb("raw", [P, 3, WPART])
        w_hi, w_lo, w_at = [], [], []
        for b in range(2):
            t, at = place(f"w_hi{b}", [P, 3, WPART], F32R)
            w_hi.append(t)
            w_at.append(at)
            w_lo.append(sb(f"w_lo{b}", [P, 3, WPART], F32R))
        h_hi, h_at = place("h_hi", [P, JH, SLOT], F32R)
        h_lo = sb("h_lo", [P, JH, SLOT], F32R)
        xs_hi, xs_at = place("xs_hi", [P, 2, KD, SLOT], F32R)
        xs_lo = sb("xs_lo", [P, 2, KD, SLOT], F32R)
        x_rows, rows_at = place("x_rows", [P, 2, ST, D])
        y_rows = sb("y_rows", [P, 2, ST, D])
        silu = sb("silu", [P, 2, 2, SLOT])
        h32 = sb("h32", [P, 2, 2, SLOT])

        z_all = sb("z_all", [P, TILES, D], at=w_at[1])
        hT_at = w_at[1] + 4 * TILES * D
        hT_hi = sb("hT_hi", [P, 2, KD, CH], F32R, at=hT_at)
        hT_lo = sb("hT_lo", [P, 2, KD, CH], F32R, at=hT_at + 8 * KD * CH)
        a_sb = sb("a_sb", [P, 2, KD, CH], at=h_at)
        y_sb = sb("y_sb", [P, 2, KD, CH], at=h_at + 8 * KD * CH)
        w_nat = sb("w_nat", [P, 3 * KD, D], at=h_at)
        wT_32 = sb("wT_32", [P, KD, 3 * D], at=h_at + 8 * KD * CH)
        wT_hi = sb("wT_hi", [P, KD, 3 * D], F32R, at=rows_at)
        wT_lo = sb("wT_lo", [P, KD, 3 * D], F32R, at=rows_at + 12 * KD * D)
        zT = sb("zT", [P, KD, CH], at=xs_at)
        zT_last = sb("zT_last", [P, KD, CH], at=hT_at)
        incl = sb("incl", [P, EP, TILES], at=hT_at + 8 * KD * CH)
        cmp = sb("cmp", [P, EP, THR], at=hT_at + 8 * KD * CH + 1024)
        owner_c = sb("owner_c", [1, ROUTED, E], at=hT_at + 8 * KD * CH + 2048)
        GR = 8
        got = sb("got", [P, GR, TOP, D], at=w_at[0])

        ident = sb("ident", [P, P])
        below = sb("below", [P, P])
        ones = sb("ones", [P, P])
        zeros = sb("zeros", [P, D])
        eps = sb("eps", [P, CT])
        power = sb("power", [P, CT])
        r_nat = sb("r_nat", [E, D])
        rT = sb("rT", [P, KD, EP])
        g_nat = sb("g_nat", [KD, P])
        gT = sb("gT", [P, KD])
        stats1 = sb("stats1", [P, CT, 6])
        stats2 = sb("stats2", [P, CT, 6])
        mv1 = sb("mv1", [P, TILES, 2])
        mv2 = sb("mv2", [P, TILES, 2])
        scale1 = sb("scale1", [P, TILES])
        bias1 = sb("bias1", [P, TILES])
        scale2 = sb("scale2", [P, TILES])
        p_var, p_rstd, p_len = (sb(n, [P, CT]) for n in ("p_var", "p_rstd", "p_len"))
        state = sb("state", [P, KD])
        iota_i = sb("iota_i", [P, 64], I32)
        iota_f = sb("iota_f", [P, 64])
        DESC, SLOTS, THRS = iota_f[:, 0:EP], iota_f[0:1, EP:EP + ROUTED], iota_f[:, 48:48 + THR]
        assert EP + ROUTED <= 48 and THR <= 16
        logits = sb("logits", [P, TILES, EP])
        first = sb("first", [P, TOP, TILES, EP])
        tmp = sb("tmp", [P, TILES, EP])
        count = sb("count", [P, EP, TILES])
        keep = sb("keep", [P, EP, TILES])
        top = sb("top", [P, TOP, TILES])
        col = sb("col", [P, TILES])
        gap = sb("gap", [P, TILES])
        mix = sb("mix", [P, TOP, TILES])
        n_slots = sb("n_slots", [P, EP])
        s_incl = sb("s_incl", [P, EP])
        s_base = sb("s_base", [P, EP])
        pos_f = sb("pos_f", [P, TILES])
        pos = sb("pos", [P, TOP, TILES], I32)
        owner_f = sb("owner_f", [1, ROUTED])
        owner = sb("owner", [1, ROUTED], I32)
        assert base[0] <= nc.sbuf_usable_end, base[0]

        ps = ctx.enter_context(nc.psum_tensor("ps", [P, 8, 512], F32))

        def sem(name):
            return ctx.enter_context(nc.semaphore(name))

        NC = N // CH
        x_in = [sem(f"x_in{g}") for g in range(NC)]
        small_in = sem("small_in")
        raw_in = [sem(f"raw_in{k}") for k in range(3)]
        consts = sem("consts")
        pool_step = sem("pool_step")
        dve_step = sem("dve_step")
        prep = sem("prep")
        prep_done = sem("prep_done")
        wT_split = sem("wT_split")
        mv1_ready, mv2_ready = sem("mv1_ready"), sem("mv2_ready")
        scaled1 = sem("scaled1")
        h_ready1 = sem("h_ready1")
        hT_psum = sem("hT_psum")
        hT_rounded = sem("hT_rounded")
        hT_split = sem("hT_split")
        a_psum, kv_psum, q_psum = sem("a_psum"), sem("kv_psum"), sem("q_psum")
        a_ready = sem("a_ready")
        y_ready = sem("y_ready")
        o_ready = sem("o_ready")
        o_psum = sem("o_psum")
        res_ready = sem("res_ready")
        z_ready = sem("z_ready")
        z_out = [sem(f"z_out{g}") for g in range(NC)]
        zT_psum = sem("zT_psum")
        zT_ready = sem("zT_ready")
        lg_psum = sem("lg_psum")
        lg_ready = sem("lg_ready")
        zeros_made = sem("zeros_made")
        zero_in = sem("zero_in")
        hot = sem("hot")
        pre_psum = sem("pre_psum")
        gap_ready = sem("gap_ready")
        mix_ready = sem("mix_ready")
        routed = sem("routed")
        scat = sem("scat")
        x_ld = [sem("x_ld0"), sem("x_ld1")]
        xT_psum = sem("xT_psum")
        xhi_ready = sem("xhi_ready")
        x_split = sem("x_split")
        whi_ready = [sem(f"whi_ready{k}") for k in range(3)]
        wlo_ready = [sem(f"wlo_ready{k}") for k in range(3)]
        gu_psum = sem("gu_psum")
        silu_ready = sem("silu_ready")
        gated = sem("gated")
        hhi_ready = sem("hhi_ready")
        h_ready = sem("h_ready")
        down_psum = sem("down_psum")
        down_free = sem("down_free")
        y_out = [sem("y_out0"), sem("y_out1")]
        got_in = [sem(f"got_in{k}") for k in range(GR)]
        mixed = sem("mixed")
        outs = sem("outs")

        POOL_LO = (0, 2)
        NB0 = SA + ROUTED

        block = ctx.enter_context(nc.Block())

        def raw_rows(gate, up, down):
            return (gate.rearrange("(k p) h -> p k h", p=P), up.rearrange("(k p) h -> p k h", p=P),
                    down.rearrange("(j p) d -> p j d", p=P))

        raw_v = [raw[:, 0, :].rearrange("p (k h) -> p k h", k=KD),
                 raw[:, 1, :].rearrange("p (k h) -> p k h", k=KD),
                 raw[:, 2, :].rearrange("p (j d) -> p j d", j=JH)]

        @block.sync
        def _(sp):
            for g in range(NC):
                sp.dma_start(resid[:, g * CT:(g + 1) * CT, :], x_t[:, g * CT:(g + 1) * CT, :]
                             ).then_inc(x_in[g], 16)
            for k, src in enumerate(raw_rows(sw_gate[0], sw_up[0], sw_down[0])):
                sp.dma_start(raw_v[k], src).then_inc(raw_in[k], 16)

            z_v = z_dram.rearrange("(g k p) d -> g p k d", p=P, k=CT)

            def store_z(g):
                sp.wait_ge(z_ready, g + 1)
                sp.dma_start(z_v[g], z_all[:, g * CT:(g + 1) * CT, :]).then_inc(z_out[g], 16)

            for g in range(NC - 1):
                store_z(g)

            def load_x(n, slot, dram, par, at):
                sp.wait_ge(xT_psum, n + 1)
                sp.dma_start(x_rows[:, par, :, :], rows_of(dram, slot)).then_inc(x_ld[par], 16)

            def load_w(sources, m):
                for k, src in enumerate(sources):
                    sp.wait_ge(wlo_ready[k], m)
                    sp.dma_start(raw_v[k], src).then_inc(raw_in[k], 16)

            def load_expert(r, m):
                e = sp.value_load(owner[0:1, bass.ds(r, 1)], min_val=0, max_val=E - 1)
                def of(w):
                    return w[bass.ds(e, 1)].rearrange("a r c -> (a r) c")
                load_w(raw_rows(of(w_gate), of(w_up), of(w_down)), m)

            sp.wait_ge(q_psum, NC)
            sp.wait_ge(z_out[0], 16)
            load_x(0, 0, z_dram, 0, 0)
            load_x(1, 1, z_dram, 1, 0)
            store_z(NC - 1)
            for g in range(1, NC):
                sp.wait_ge(z_out[g], 16)
            for u in range(2):
                load_x(2 + u, 2 + u, z_dram, u, 0)
            sp.wait_ge(routed, 2)
            load_expert(0, 1)
            with sp.Fori(2, SA // 2) as i:
                for u in range(2):
                    load_x(i * 2 + u, i * 2 + u, z_dram, u, i)
            sp.wait_ge(scat, 16 * TOP * TILES)
            with sp.Fori(0, ROUTED // 2 - 1) as i:
                for u in range(2):
                    load_x(i * 2 + (SA + u), i * 2 + u, sorted_dram, u, i)
                    load_expert(i * 2 + (u + 1), i * 2 + (u + 2))
            load_x(NB0 - 2, ROUTED - 2, sorted_dram, 0, 0)
            load_expert(ROUTED - 1, ROUTED)
            load_x(NB0 - 1, ROUTED - 1, sorted_dram, 1, 0)
            load_w(raw_rows(sw_gate[0], sw_up[0], sw_down[0]), ROUTED + 1)
            for u in range(2):
                load_x(NB0 + u, SA + u, z_dram, u, 0)

            def store(i):
                sp.wait_ge(mixed, i * 2 * GR + 2 * GR)
                sp.wait_ge(down_free, i * 2 + (NB0 + 3))
                for half in range(2):
                    t0 = i * CT + half * (TILES // 2)
                    sp.dma_start(out_t[:, bass.ds(t0, CT), :], resid[:, bass.ds(t0, CT), :]
                                 ).then_inc(outs, 16)

            with sp.Fori(0, SBN // 2 - 1) as i:
                for u in range(2):
                    load_x(i * 2 + (NB0 + 2 + u), i * 2 + (SA + 2 + u), z_dram, u, i)
                store(i)
            store(SBN // 2 - 1)
            sp.wait_ge(outs, 16 * SBN)
            for u in range(2):
                sp.wait_ge(y_out[u], 16 + 16 * (ROUTED // 2))
            sp.wait_ge(zero_in, 16 * ZEROS)

        @block.gpsimd
        def _(pool):
            made = [0]

            def own(ins):
                made[0] += 1
                ins.then_inc(pool_step, 1)

            def step(ins):
                own(ins)
                pool.wait_ge(pool_step, made[0])

            own(pool.memset(ident[:, :], 0.0))
            own(pool.memset(below[:, :], 1.0))
            own(pool.memset(ones[:, :], 1.0))
            own(pool.memset(eps[:, :], EPS))
            own(pool.memset(power[:, :], -0.5))
            own(pool.iota(iota_i[:, 0:EP], pattern=[[-1, EP]], base=EP, channel_multiplier=0))
            own(pool.iota(iota_i[:, EP:48], pattern=[[1, 48 - EP]], base=0, channel_multiplier=0))
            own(pool.iota(iota_i[:, 48:64], pattern=[[SLOT, 16]], base=0, channel_multiplier=0))
            pool.wait_ge(pool_step, made[0])
            pool.affine_select(out=ident[:, :], in_=ident[:, :], compare_op=ALU.not_equal, fill=1.0,
                               base=0, pattern=[[-1, P]], channel_multiplier=1).then_inc(consts, 1)
            pool.affine_select(out=below[:, :], in_=below[:, :], compare_op=ALU.is_gt, fill=0.0,
                               base=0, pattern=[[1, P]], channel_multiplier=-1).then_inc(consts, 1)
            pool.tensor_copy(iota_f[:, :], iota_i[:, :]).then_inc(consts, 1)

            def inv_sqrt(out, a):
                step(pool.tensor_tensor(out, a, power[:, :], ALU.pow))

            def scales1(g):
                ts = slice(g * CT, (g + 1) * CT)
                pool.wait_ge(mv1_ready, g + 1)
                var, mean = mv1[:, ts, 1], mv1[:, ts, 0]
                step(pool.tensor_tensor(p_var[:, :], var, eps[:, :], ALU.add))
                inv_sqrt(p_rstd[:, :], p_var[:, :])
                step(pool.tensor_tensor(p_len[:, :], var, p_rstd[:, :], ALU.mult))
                step(pool.tensor_tensor(p_len[:, :], p_len[:, :], p_rstd[:, :], ALU.mult))
                step(pool.tensor_scalar(p_len[:, :], p_len[:, :], float(D), TINY2, ALU.mult, ALU.max))
                inv_sqrt(p_var[:, :], p_len[:, :])
                step(pool.tensor_tensor(p_var[:, :], p_var[:, :], p_rstd[:, :], ALU.mult))
                step(pool.tensor_scalar(scale1[:, ts], p_var[:, :], float(D) ** 0.5, None, ALU.mult))
                step(pool.tensor_tensor(p_len[:, :], mean, scale1[:, ts], ALU.mult))
                pool.tensor_scalar(bias1[:, ts], p_len[:, :], -1.0, None, ALU.mult
                                   ).then_inc(scaled1, 1)
                pool.wait_ge(scaled1, g + 1)

            def z_rows(g):
                ts = slice(g * CT, (g + 1) * CT)
                pool.wait_ge(mv2_ready, g + 1)
                step(pool.tensor_tensor(p_var[:, :], mv2[:, ts, 1], eps[:, :], ALU.add))
                inv_sqrt(scale2[:, ts], p_var[:, :])
                for t in range(g * CT, (g + 1) * CT):
                    last = pool.tensor_scalar(z_all[:, t, :], resid[:, t, :], mv2[:, t, 0:1],
                                              scale2[:, t:t + 1], ALU.subtract, ALU.mult)
                last.then_inc(z_ready, 1)

            def split_lo(k, m, buf):
                pool.wait_ge(whi_ready[k], m + 1)
                pool.tensor_tensor(w_lo[buf][:, k, :], raw[:, k, :], w_hi[buf][:, k, :].bitcast(F32),
                                   ALU.subtract).then_inc(wlo_ready[k], 1)

            pool.wait_ge(pool_step, made[0])
            for g in range(3):
                scales1(g)
            for g in range(NC):
                if g + 3 < NC:
                    scales1(g + 3)
                if g >= 1:
                    z_rows(g - 1)
                if 4 <= g < 7:
                    split_lo(g - 4, 0, 0)
            z_rows(NC - 1)
            pool.wait_ge(z_ready, NC)
            pool.wait_ge(zero_in, ZEROS * 16)
            pool.wait_ge(routed, 2)
            for t in range(TILES):
                for k in range(TOP):
                    pool.indirect_dma_start(
                        sorted_dram, bass.IndirectOffsetOnAxis(ap=pos[:, k, t:t + 1], axis=0),
                        z_all[:, t, :], None, bounds_check=ROUTED * SLOT - 1).then_inc(scat, 16)
            for k in POOL_LO:
                split_lo(k, 1, 1)
            with pool.Fori(0, ROUTED // 2) as i:
                for u in range(2):
                    for k in POOL_LO:
                        split_lo(k, i * 2 + (u + 2), u)

            for u in range(2):
                pool.wait_ge(y_out[u], 16 + 16 * (ROUTED // 2))
            for i in range(TILES // GR):
                for r in range(GR):
                    t = i * CT + r % CT + (r // CT) * (TILES // 2)
                    if i:
                        pool.wait_ge(mixed, TOP * ((i - 1) * GR + r + 1))
                    for k in range(TOP):
                        pool.indirect_dma_start(
                            got[:, r, k, :], None, y_dram,
                            bass.IndirectOffsetOnAxis(ap=pos[:, k, t:t + 1], axis=0),
                            bounds_check=ROUTED * SLOT - 1).then_inc(got_in[r], 16)

        @block.scalar
        def _(act):
            for k, (dst, src) in enumerate((
                    (w_nat[:, :, :], w_qkva.rearrange("(e p) d -> p e d", p=P)),
                    (g_nat[:, :], gamma.rearrange("(k p) -> k p", p=P)),
                    (r_nat[:, :], router_w))):
                act.dma_start(dst, src).then_inc(small_in, 16)
            act.wait_ge(prep, 1)
            act.activation(gT[:, :], ps[:, 6, 0:KD], ACT.Copy).then_inc(prep_done, 1)
            act.activation(rT[:, :, 0:E], ps[:, 7, 0:KD * E].rearrange("p (k e) -> p k e", k=KD),
                           ACT.Copy).then_inc(prep_done, 1)
            act.wait_ge(prep_done, 1)
            for k in range(KD):
                act.activation(wT_32[:, k, :].rearrange("p (a n) -> p a n", a=2),
                               ps[:, 2 * k:2 * k + 2, 0:3 * P], ACT.Copy,
                               scale=gT[:, k:k + 1]).then_inc(prep_done, 1)
            act.wait_ge(prep_done, 2 + KD)
            act.activation(wT_hi[:, :, :], wT_32[:, :, :], ACT.Copy).then_inc(prep_done, 1)

            def h_rows(g):
                act.wait_ge(scaled1, g + 1)
                for t in range(g * CT, (g + 1) * CT):
                    last = act.activation(z_all[:, t, :], resid[:, t, :], ACT.Identity,
                                          scale=scale1[:, t:t + 1], bias=bias1[:, t:t + 1])
                last.then_inc(h_ready1, 1)

            def h_hi_part(g):
                act.wait_ge(hT_psum, g + 1)
                if g >= 2:
                    act.wait_ge(q_psum, g - 1)
                act.activation(hT_hi[:, g % 2, :, :], ps[:, 0:2, :], ACT.Copy
                               ).then_inc(hT_rounded, 1)

            def zT_copy(g, dst, bank):
                act.wait_ge(zT_psum, g + 1)
                if g >= 1:
                    act.wait_ge(lg_psum, g)
                act.activation(dst[:, :, :], ps[:, bank:bank + 2, :], ACT.Copy).then_inc(zT_ready, 1)

            h_rows(0)
            h_rows(1)
            h_hi_part(0)
            for g in range(NC):
                act.wait_ge(a_psum, g + 1)
                if g >= 2:
                    act.wait_ge(y_ready, g - 1)
                at = 2 + 2 * (g % 2)
                act.activation(a_sb[:, g % 2, :, :], ps[:, at:at + 2, :], ACT.Sigmoid
                               ).then_inc(a_ready, 1)
                if g + 2 < NC:
                    h_rows(g + 2)
                if g + 1 < NC:
                    h_hi_part(g + 1)
                if g >= 2:
                    zT_copy(g - 2, zT, 0)
                if g == 0:
                    act.wait_ge(zeros_made, 1)
                    for x_g in x_in:
                        act.wait_ge(x_g, 16)
                    rows = sorted_dram.rearrange("(z k p) d -> z p k d", p=P, z=ZEROS)
                    for z in range(ZEROS):
                        act.dma_start(rows[z], zeros[:, :].unsqueeze(1).broadcast_to(
                            [P, rows.shape[2], D])).then_inc(zero_in, 16)
                if 4 <= g < 7:
                    act.wait_ge(raw_in[g - 4], 16)
                    act.activation(w_hi[0][:, g - 4, :], raw[:, g - 4, :], ACT.Copy
                                   ).then_inc(whi_ready[g - 4], 1)
            zT_copy(NC - 2, zT, 0)

            def x_hi(n, par):
                act.wait_ge(xT_psum, n + 3)
                act.activation(xs_hi[:, par, :, :], ps[:, 6, :].rearrange("p (k n) -> p k n", k=KD),
                               ACT.Copy).then_inc(xhi_ready, 1)

            def slot(n, u, r=None, last=False):
                for p in range(PAIRS):
                    q = n * PAIRS + p
                    par = p % 2
                    act.wait_ge(gu_psum, q + 1)
                    act.activation(silu[:, par, :, :], ps[:, 2 * par:2 * par + 2, 0:SLOT], ACT.Silu
                                   ).then_inc(silu_ready, 1)
                    act.wait_ge(gated, q + 3)
                    if p == 0:
                        act.wait_ge(down_psum, n + 1)
                    act.activation(h_hi[:, 2 * p:2 * p + 2, :], h32[:, par, :, :], ACT.Copy
                                   ).then_inc(hhi_ready, 1)
                if not last:
                    x_hi(n + 1, 1 - u)
                if r is not None:
                    act.wait_ge(down_psum, n + 2)
                    act.wait_ge(y_out[u], r)
                    act.activation(y_rows[:, u, :, :], ps[:, 4:6, 0:D], ACT.Copy
                                   ).then_inc(down_free, 1)
                    act.wait_ge(down_free, n + 2)
                    act.dma_start(rows_of(y_dram, n - SA), y_rows[:, u, :, :]).then_inc(y_out[u], 16)

            x_hi(0, 0)
            slot(0, 0)
            zT_copy(NC - 1, zT_last, 4)
            slot(1, 1)
            act.wait_ge(gap_ready, 1)
            act.activation(mix[:, 0, :], gap[:, :], ACT.Sigmoid).then_inc(mix_ready, 1)
            act.activation(mix[:, 1, :], gap[:, :], ACT.Sigmoid, scale=-1.0).then_inc(mix_ready, 1)
            with act.Fori(1, SA // 2) as i:
                for u in range(2):
                    slot(i * 2 + u, u)
            with act.Fori(0, ROUTED // 2) as i:
                for u in range(2):
                    slot(i * 2 + (SA + u), u, r=i * 16 + 16)
            with act.Fori(0, SBN // 2 - 1) as i:
                for u in range(2):
                    slot(i * 2 + (NB0 + u), u)
            slot(NB0 + SBN - 2, 0)
            slot(NB0 + SBN - 1, 1, last=True)

        @block.tensor
        def _(pe):
            pe.wait_ge(consts, 3)
            pe.wait_ge(small_in, 48)
            pe.transpose(ps[:, 6, 0:KD], g_nat[:, :], ident[0:KD, 0:KD])
            for k in range(KD):
                pe.transpose(ps[:, 7, k * E:k * E + E], r_nat[:, k * P:(k + 1) * P], ident[0:E, 0:E])
            for k in range(KD):
                for e in range(3 * KD):
                    last = pe.transpose(ps[:, 2 * k + e // 3, (e % 3) * P:(e % 3 + 1) * P],
                                        w_nat[:, e, k * P:(k + 1) * P], ident[:, :])
            last.then_inc(prep, 1)
            pe.wait_ge(prep_done, 2 + KD)

            def turn(g, bank, signal):
                for kd in range(KD):
                    for k in range(CT):
                        last = pe.transpose(ps[:, bank + kd, k * P:(k + 1) * P],
                                            z_all[:, g * CT + k, kd * P:(kd + 1) * P], ident[:, :])
                last.then_inc(signal, 1)

            def turn_h(g):
                pe.wait_ge(h_ready1, g + 1)
                if g >= 1:
                    pe.wait_ge(hT_split, g)
                if g >= 4:
                    pe.wait_ge(lg_ready, g - 3)
                turn(g, 0, hT_psum)

            def turn_z(g, bank):
                pe.wait_ge(z_ready, g + 1)
                if g >= 1:
                    pe.wait_ge(lg_ready, g)
                turn(g, bank, zT_psum)

            def route(g, src, bank):
                pe.wait_ge(zT_ready, g + 1)
                for k in range(CT):
                    for kd in range(KD):
                        last = pe.matmul(ps[:, bank, k * EP:k * EP + E],
                                         src[:, kd, k * P:(k + 1) * P], rT[:, kd, 0:E],
                                         start=kd == 0, stop=kd == KD - 1)
                last.then_inc(lg_psum, 1)

            def project(g, part, bank, signal):
                c = g % 2
                for e in range(KD):
                    at = (part * KD + e) * P
                    terms = [(w, h, kd) for kd in range(KD)
                             for w, h in ((wT_hi, hT_hi), (wT_hi, hT_lo), (wT_lo, hT_hi))]
                    for i, (w, h, kd) in enumerate(terms):
                        last = pe.matmul(ps[:, bank + e, :], w[:, kd, at:at + P], h[:, c, kd, :],
                                         start=i == 0, stop=i == len(terms) - 1)
                last.then_inc(signal, 1)

            def turn_back(g):
                pe.wait_ge(o_ready, g + 1)
                if g >= 1:
                    pe.wait_ge(res_ready, g)
                for k in range(CT):
                    for e in range(KD):
                        at = (k % 2) * D + e * P
                        last = pe.transpose(ps[:, 6 + k // 2, at:at + P],
                                            y_sb[:, g % 2, e, k * P:(k + 1) * P], ident[:, :])
                last.then_inc(o_psum, 1)

            turn_h(0)
            pe.wait_ge(wT_split, 1)
            for g in range(NC):
                one = 2 + 2 * (g % 2)
                two = 6 - one
                pe.wait_ge(hT_split, g + 1)
                if g >= 1:
                    pe.wait_ge(y_ready, g)
                project(g, 2, one, a_psum)
                if g >= 1:
                    turn_back(g - 1)
                if g >= 3:
                    route(g - 3, zT, 0)
                if g >= 1:
                    pe.wait_ge(o_ready, g)
                project(g, 1, two, kv_psum)
                if g + 1 < NC:
                    turn_h(g + 1)
                pe.wait_ge(a_ready, g + 1)
                project(g, 0, one, q_psum)
                if g >= 2:
                    pe.wait_ge(hT_split, min(g + 2, NC))
                    turn_z(g - 2, 0)
            route(NC - 3, zT, 0)
            turn_z(NC - 2, 0)
            turn_back(NC - 1)
            route(NC - 2, zT, 0)
            pe.wait_ge(lg_ready, NC - 1)
            pe.wait_ge(res_ready, NC)

            def ranks():
                pe.wait_ge(hot, 1)
                flat = tmp[:, :, :].rearrange("p t e -> p (t e)")
                pe.matmul(ps[:, 7, 0:TILES * EP], below[:, :], flat, start=True, stop=True)
                pe.matmul(ps[:, 7, TILES * EP:2 * TILES * EP], ones[:, :], flat, start=True, stop=True
                          ).then_inc(pre_psum, 1)

            def turn_x(n, u, nth):
                pe.wait_ge(x_ld[u], nth)
                for t in range(ST):
                    for kd in range(KD):
                        last = pe.transpose(ps[:, 6, kd * SLOT + t * P:kd * SLOT + (t + 1) * P],
                                            x_rows[:, u, t, kd * P:(kd + 1) * P], ident[:, :])
                last.then_inc(xT_psum, 1)

            def slot(n, u, buf, nth, m=None, last_slot=False, between=()):
                pe.wait_ge(x_split, n + 1)
                if m is not None:
                    for k in range(2):
                        pe.wait_ge(wlo_ready[k], m + 1)
                hi, lo = w_hi[buf], w_lo[buf]
                for p in range(PAIRS):
                    q = n * PAIRS + p
                    pe.wait_ge(gated, q + 1)
                    for j in (2 * p, 2 * p + 1):
                        for part in range(2):
                            o = ps[:, 2 * (p % 2) + j % 2, part * SLOT:(part + 1) * SLOT]
                            at = [kd * H + j * P for kd in range(KD)]
                            terms = [(w, xx, kd) for kd in range(KD)
                                     for w, xx in ((hi, xs_hi), (hi, xs_lo), (lo, xs_hi))]
                            for i, (w, xx, kd) in enumerate(terms):
                                last = pe.matmul(o, w[:, part, at[kd]:at[kd] + P], xx[:, u, kd, :],
                                                 start=i == 0, stop=i == len(terms) - 1)
                    last.then_inc(gu_psum, 1)
                    if p in between:
                        between[p]()
                if not last_slot:
                    turn_x(n + 1, 1 - u, nth)
                if m is not None:
                    pe.wait_ge(wlo_ready[2], m + 1)
                pe.wait_ge(down_free, n + 1)
                for p in range(PAIRS):
                    pe.wait_ge(h_ready, n * PAIRS + (p + 3))
                    for j in (2 * p, 2 * p + 1):
                        for t in range(ST):
                            terms = ((h_hi, hi), (h_hi, lo), (h_lo, hi))
                            for i, (hh, w) in enumerate(terms):
                                last = pe.matmul(ps[:, 4 + t, 0:D], hh[:, j, t * P:(t + 1) * P],
                                                 w[:, 2, j * D:(j + 1) * D],
                                                 start=j == 0 and i == 0,
                                                 stop=j == JH - 1 and i == len(terms) - 1)
                last.then_inc(down_psum, 1)

            turn_x(0, 0, 16)
            for k in range(3):
                pe.wait_ge(wlo_ready[k], 1)
            slot(0, 0, 0, 16)
            pe.wait_ge(down_free, 2)
            turn_z(NC - 1, 4)
            slot(1, 1, 0, 32, between={0: lambda: route(NC - 1, zT_last, 7), 3: ranks})
            with pe.Fori(1, SA // 2) as i:
                slot(i * 2, 0, 0, i * 16 + 16)
                slot(i * 2 + 1, 1, 0, i * 16 + 32)
            R0 = SA // 2
            with pe.Fori(0, ROUTED // 2) as i:
                slot(i * 2 + SA, 0, 1, i * 16 + 16 * (R0 + 1), m=i * 2 + 1)
                slot(i * 2 + (SA + 1), 1, 0, i * 16 + 16 * (R0 + 2), m=i * 2 + 2)
            B0 = NB0 // 2
            for k in range(3):
                pe.wait_ge(wlo_ready[k], ROUTED + 2)
            with pe.Fori(0, SBN // 2 - 1) as i:
                slot(i * 2 + NB0, 0, 1, i * 16 + 16 * (B0 + 1))
                slot(i * 2 + (NB0 + 1), 1, 1, i * 16 + 16 * (B0 + 2))
            slot(NB0 + SBN - 2, 0, 1, 16 * (B0 + SBN // 2))
            slot(NB0 + SBN - 1, 1, 1, None, last_slot=True)

        @block.vector
        def _(dve):
            for s, n in ((xT_psum, 2), (gated, 2), (h_ready, 2), (down_psum, 1), (down_free, 1), (y_out[0], 16), (y_out[1], 16)):
                dve.sem_inc(s, n)
            made = [0]

            def step(ins):
                made[0] += 1
                ins.then_inc(dve_step, 1)
                dve.wait_ge(dve_step, made[0])

            dve.memset(zeros[:, :], 0.0).then_inc(zeros_made, 1)
            dve.memset(logits[:, :, E:EP], LOWEST)
            dve.memset(keep[:, :, 1:TILES], 1.0)
            step(dve.memset(keep[:, :, 0:1], 0.0))

            def statistics(g, stats, mv, signal):
                if g >= 1:
                    dve.wait_ge(signal, g)
                for k in range(CT):
                    last = dve.bn_stats(stats[:, k, :], resid[:, g * CT + k, :])
                step(last)
                for k in range(CT):
                    last = dve.bn_aggr(mv[:, g * CT + k, :], stats[:, k, :])
                last.then_inc(signal, 1)

            def statistics1(g):
                dve.wait_ge(x_in[g], 16)
                statistics(g, stats1, mv1, mv1_ready)

            def h_lo_part(g):
                dve.wait_ge(hT_rounded, g + 1)
                dve.tensor_tensor(hT_lo[:, g % 2, :, :], ps[:, 0:2, :],
                                  hT_hi[:, g % 2, :, :].bitcast(F32), ALU.subtract
                                  ).then_inc(hT_split, 1)

            def residual(g):
                dve.wait_ge(o_psum, g + 1)
                rows = resid[:, g * CT:(g + 1) * CT, :]
                dve.tensor_tensor(rows, ps[:, 6:8, :].rearrange("p b (k d) -> p (b k) d", d=D), rows,
                                  ALU.add).then_inc(res_ready, 1)
                dve.wait_ge(res_ready, g + 1)
                statistics(g, stats2, mv2, mv2_ready)

            def take_logits(g, bank):
                dve.wait_ge(lg_psum, g + 1)
                dve.tensor_copy(logits[:, g * CT:(g + 1) * CT, 0:E],
                                ps[:, bank, 0:CT * EP].rearrange("p (k e) -> p k e", e=EP)[:, :, 0:E]
                                ).then_inc(lg_ready, 1)

            def scan(g):
                c, kv = g % 2, 4 - 2 * (g % 2)
                dve.wait_ge(a_ready, g + 1)
                dve.wait_ge(kv_psum, g + 1)
                if g >= 2:
                    dve.wait_ge(o_psum, g - 1)
                for e in range(KD):
                    last = dve.tensor_tensor_scan(y_sb[:, c, e, :], a_sb[:, c, e, :], ps[:, kv + e, :],
                                                  state[:, e:e + 1] if c else 0.0, ALU.mult, ALU.add)
                last.then_inc(y_ready, 1)
                dve.wait_ge(y_ready, g + 1)
                if c == 0:
                    step(dve.tensor_copy(state[:, :], y_sb[:, c, :, CH - 1]))

            def times_q(g):
                c, q = g % 2, 2 + 2 * (g % 2)
                dve.wait_ge(q_psum, g + 1)
                dve.tensor_tensor(y_sb[:, c, :, :], ps[:, q:q + 2, :], y_sb[:, c, :, :], ALU.mult
                                  ).then_inc(o_ready, 1)

            for g in range(3):
                statistics1(g)
            dve.wait_ge(prep_done, 3 + KD)
            dve.tensor_tensor(wT_lo[:, :, :], wT_32[:, :, :], wT_hi[:, :, :].bitcast(F32), ALU.subtract
                              ).then_inc(wT_split, 1)
            h_lo_part(0)
            dve.wait_ge(wT_split, 1)
            for g in range(NC):
                if g >= 1:
                    residual(g - 1)
                if g >= 3:
                    take_logits(g - 3, 0)
                scan(g)
                if g + 1 < NC:
                    h_lo_part(g + 1)
                times_q(g)
                if g + 3 < NC:
                    statistics1(g + 3)
            take_logits(NC - 3, 0)
            residual(NC - 1)
            take_logits(NC - 2, 0)

            def choose():
                def over_experts(a):
                    return a.unsqueeze(2).broadcast_to([P, TILES, EP])

                desc = DESC.unsqueeze(1).broadcast_to([P, TILES, EP])
                dve.wait_ge(lg_ready, NC)
                dve.wait_ge(consts, 3)
                for k in range(TOP):
                    step(dve.tensor_reduce(top[:, k, :], logits[:, :, :], AX_X, ALU.max))
                    step(dve.tensor_tensor(tmp[:, :, :], logits[:, :, :], over_experts(top[:, k, :]),
                                           ALU.is_equal))
                    step(dve.tensor_tensor(tmp[:, :, :], tmp[:, :, :], desc, ALU.mult))
                    step(dve.tensor_reduce(col[:, :], tmp[:, :, :], AX_X, ALU.max))
                    step(dve.tensor_tensor(first[:, k, :, :], over_experts(col[:, :]), desc, ALU.is_equal))
                    if k == 0:
                        step(dve.scalar_tensor_tensor(out=logits[:, :, :], in0=first[:, 0, :, :],
                                                      scalar=LOWEST, in1=logits[:, :, :],
                                                      op0=ALU.mult, op1=ALU.add))
                dve.tensor_tensor(gap[:, :], top[:, 0, :], top[:, 1, :], ALU.subtract).then_inc(gap_ready, 1)
                dve.tensor_tensor(tmp[:, :, :], first[:, 0, :, :], first[:, 1, :, :], ALU.add
                                  ).then_inc(hot, 1)

            def rank():
                dve.wait_ge(pre_psum, 1)
                before = ps[:, 7, 0:TILES * EP].rearrange("p (t e) -> p t e", e=EP)
                total = ps[:, 7, TILES * EP:2 * TILES * EP].rearrange("p (t e) -> p e t", e=EP)
                step(dve.tensor_copy(count[:, :, :], total))
                step(dve.tensor_tensor_scan(incl[:, :, :].rearrange("p e t -> p (e t)"),
                                            keep[:, :, :].rearrange("p e t -> p (e t)"),
                                            count[:, :, :].rearrange("p e t -> p (e t)"),
                                            0.0, ALU.mult, ALU.add))
                step(dve.tensor_tensor(cmp[:, :, :], incl[:, :, TILES - 1:TILES].broadcast_to([P, EP, THR]),
                                       THRS.unsqueeze(1).broadcast_to([P, EP, THR]), ALU.is_gt))
                step(dve.tensor_reduce(n_slots[:, :], cmp[:, :, :], AX_X, ALU.add))
                step(dve.tensor_tensor_scan(s_incl[:, :], ones[:, 0:EP], n_slots[:, :], 0.0,
                                            ALU.mult, ALU.add))
                step(dve.tensor_tensor(s_base[:, :], s_incl[:, :], n_slots[:, :], ALU.subtract))
                step(dve.tensor_scalar(s_base[:, :], s_base[:, :], float(SLOT), None, ALU.mult))
                step(dve.tensor_tensor(count[:, :, :], incl[:, :, :], count[:, :, :], ALU.subtract))
                step(dve.tensor_tensor(count[:, :, :], count[:, :, :],
                                       s_base[:, :].unsqueeze(2).broadcast_to([P, EP, TILES]), ALU.add))
                step(dve.tensor_tensor(tmp[:, :, :], before, count[:, :, :].rearrange("p e t -> p t e"),
                                       ALU.add))
                for k in range(TOP):
                    step(dve.tensor_tensor(first[:, k, :, :], first[:, k, :, :], tmp[:, :, :], ALU.mult))
                    step(dve.tensor_reduce(pos_f[:, :], first[:, k, :, :], AX_X, ALU.add))
                    ins = dve.tensor_copy(pos[:, k, :], pos_f[:, :])
                    if k < TOP - 1:
                        step(ins)
                ins.then_inc(routed, 1)
                dve.tensor_tensor(owner_c[:, :, :], s_incl[0:1, 0:E].unsqueeze(1).broadcast_to([1, ROUTED, E]),
                                  SLOTS.unsqueeze(2).broadcast_to([1, ROUTED, E]), ALU.is_le
                                  ).then_inc(dve_step, 1)
                made[0] += 1
                dve.wait_ge(dve_step, made[0])
                step(dve.tensor_reduce(owner_f[:, :], owner_c[:, :, :], AX_X, ALU.add))
                step(dve.tensor_scalar(owner_f[:, :], owner_f[:, :], float(E - 1), None, ALU.min))
                dve.tensor_copy(owner[:, :], owner_f[:, :]).then_inc(routed, 1)

            def x_lo(n, par):
                dve.wait_ge(xhi_ready, n + 1)
                dve.tensor_tensor(xs_lo[:, par, :, :], ps[:, 6, :].rearrange("p (k n) -> p k n", k=KD),
                                  xs_hi[:, par, :, :].bitcast(F32), ALU.subtract).then_inc(x_split, 1)

            def mix_tile(r, k, t, n_mixed, n_got):
                if k == 0:
                    dve.wait_ge(got_in[r], n_got)
                else:
                    dve.wait_ge(mixed, n_mixed)
                row = resid[:, bass.ds(t, 1), :]
                dve.scalar_tensor_tensor(out=row, in0=got[:, r, k:k + 1, :],
                                         scalar=mix[:, k, bass.ds(t, 1)], in1=row,
                                         op0=ALU.mult, op1=ALU.add).then_inc(mixed, 1)

            def split_hi(k, m, buf, load):
                dve.wait_ge(raw_in[k], load)
                dve.tensor_copy(w_hi[buf][:, k, :], raw[:, k, :]).then_inc(whi_ready[k], 1)

            def split_lo(k, m, buf):
                dve.wait_ge(whi_ready[k], m + 1)
                dve.tensor_tensor(w_lo[buf][:, k, :], raw[:, k, :], w_hi[buf][:, k, :].bitcast(F32),
                                  ALU.subtract).then_inc(wlo_ready[k], 1)

            def slot(n, u, m=None, load=None, shared=None, back=None, last=False, between=None):
                for p in range(PAIRS):
                    q = n * PAIRS + p
                    par = p % 2
                    dve.wait_ge(silu_ready, q + 1)
                    dve.wait_ge(h_ready, q + 1)
                    dve.tensor_tensor(h32[:, par, :, :], ps[:, 2 * par:2 * par + 2, SLOT:2 * SLOT],
                                      silu[:, par, :, :], ALU.mult).then_inc(gated, 1)
                    if m is not None and p < 3:
                        if p < 2:
                            dve.wait_ge(gu_psum, n * PAIRS)
                        else:
                            dve.wait_ge(down_psum, n + 1)
                        split_hi(p, m, u, load)
                    if back is not None:
                        r = u * CT + p
                        t = back * CT + (p + u * (TILES // 2))
                        done = back * (TOP * GR) + (TOP * r + 1)
                        mix_tile(r, 0, t, None, back * (16 * TOP) + 16 * TOP)
                    dve.wait_ge(hhi_ready, q + 1)
                    dve.tensor_tensor(h_lo[:, 2 * p:2 * p + 2, :], h32[:, par, :, :],
                                      h_hi[:, 2 * p:2 * p + 2, :].bitcast(F32), ALU.subtract
                                      ).then_inc(h_ready, 1)
                    if back is not None:
                        mix_tile(r, 1, t, done, None)
                    if p == 0 and between is not None:
                        between()
                if not last:
                    x_lo(n + 1, 1 - u)
                if m is not None:
                    split_lo(1, m, u)
                if shared is not None:
                    dve.wait_ge(down_psum, n + 2)
                    if back is not None:
                        dve.wait_ge(mixed, back * (TOP * GR) + TOP * CT * (u + 1))
                    rows = resid[:, bass.ds(shared, ST), :]
                    dve.tensor_tensor(rows, ps[:, 4:6, 0:D], rows, ALU.add).then_inc(down_free, 1)
                    dve.wait_ge(down_free, n + 2)

            x_lo(0, 0)
            def last_logits():
                take_logits(NC - 1, 7)
                choose()

            slot(0, 0, shared=0)
            slot(1, 1, shared=ST, between=last_logits)
            rank()
            with dve.Fori(1, SA // 2 - 1) as i:
                for u in range(2):
                    slot(i * 2 + u, u, shared=i * (2 * ST) + u * ST)
            slot(SA - 2, 0, shared=(SA - 2) * ST)
            dve.wait_ge(scat, 16 * TOP * TILES)
            slot(SA - 1, 1, m=1, load=32, shared=(SA - 1) * ST)
            with dve.Fori(0, ROUTED // 2) as i:
                for u in range(2):
                    slot(i * 2 + (SA + u), u, m=i * 2 + (2 + u), load=i * 32 + (48 + 16 * u))
            dve.wait_ge(mix_ready, TOP)
            with dve.Fori(0, SBN // 2 - 1) as i:
                for u in range(2):
                    slot(i * 2 + (NB0 + u), u, shared=i * (2 * ST) + (TILES // 2 + u * ST), back=i)
            i = SBN // 2 - 1
            for u in range(2):
                slot(i * 2 + NB0 + u, u, shared=i * 2 * ST + TILES // 2 + u * ST, back=i, last=u == 1)


_INS = ['L0_attn_x', 'L0_attn_w_qkva', 'L0_attn_gamma', 'L0_ffn_router_w', 'L0_ffn_w_gate',
        'L0_ffn_w_up', 'L0_ffn_w_down', 'L0_ffn_sw_gate', 'L0_ffn_sw_up', 'L0_ffn_sw_down']


def kernel(**inputs):
    import numpy as _np
    import concourse.bacc as _bacc
    from concourse import mybir as _mybir
    from concourse.bass_utils import run_bass_kernel_spmd as _run

    nc = _bacc.Bacc("TRN2", target_bir_lowering=False, num_devices=1)
    arrays, args = {}, []
    for name in _INS:
        a = _np.ascontiguousarray(inputs[name])
        arrays[f"in_{name}_dram"] = a
        args.append(nc.dram_tensor(f"in_{name}_dram", a.shape, _mybir.dt.from_np(a.dtype), kind="ExternalInput").ap())
    shape = inputs['L0_attn_x'].shape
    args.append(nc.dram_tensor("out_0_dram", shape, _mybir.dt.float32, kind="ExternalOutput").ap())
    preln_scan_moe_kernel(nc, *args)
    r = _run(nc, [arrays], core_ids=[0])
    return r.results[0]["out_0_dram"]
```

```python
from contextlib import ExitStack

import concourse.bass as bass
from concourse import mybir

F32 = mybir.dt.float32
F32R = mybir.dt.float32r
I32 = mybir.dt.int32
ALU = mybir.AluOpType
ACT = mybir.ActivationFunctionType
AX_X = mybir.AxisListType.X

P = 128
SLOT = 256
EPS = 1e-5
TINY2 = 1e-24
LOWEST = -3.0e38


def preln_scan_moe_kernel(nc, x, w_qkva, gamma, router_w, w_gate, w_up, w_down,
                          sw_gate, sw_up, sw_down, out):
    B, S, D = x.shape
    E, _, H = w_gate.shape
    N = B * S
    TILES = N // P
    CH = 512
    CT = CH // P
    NC = N // CH
    KD = D // P
    JH = H // P
    EP = 8
    TOP = 2
    ST = SLOT // P
    SHARED = N // SLOT
    SA = SHARED // 2
    SBN = SHARED - SA
    ROUTED = (TOP * N + E * (SLOT - 1)) // SLOT
    ROUTED += ROUTED % 2
    THR = N // SLOT
    ZEROS = 8
    PAIRS = JH // 2
    WPART = KD * H
    assert B == 4 and S == 2 * CH and KD == 2 and WPART == JH * D and SA % 2 == 0 and E < EP

    x_t = x.rearrange("b (k p) d -> p (b k) d", p=P)
    out_t = out.rearrange("b (k p) d -> p (b k) d", p=P)
    z_dram = nc.dram_tensor("z_rows", [N, D], F32).ap()
    sorted_dram = nc.dram_tensor("sorted_rows", [ROUTED * SLOT, D], F32).ap()
    y_dram = nc.dram_tensor("expert_rows", [ROUTED * SLOT, D], F32).ap()

    BK = 32
    NBK = P // BK
    LD = 16 * NBK

    def piece_of(dram, n, size, a):
        v = dram.rearrange("(s b j) (a c) -> s a j b c", b=size // BK, j=BK, a=NBK)
        return v[bass.ds(n, 1), a].rearrange("s j b c -> (s j) b c")

    def rows_of(dram, slot):
        return dram.rearrange("(s t p) d -> s p t d", p=P, t=ST)[bass.ds(slot, 1)].rearrange(
            "a p t d -> p (a t) d")

    with ExitStack() as ctx:
        base = [(nc.sbuf_base + 31) // 32 * 32]

        def place(name, shape, dtype=F32, at=None):
            free = 4
            for n in shape[1:]:
                free *= n
            if at is None:
                at = base[0]
                base[0] += (free + 31) // 32 * 32
            return nc.alloc_sbuf_tensor_at(name, shape, dtype, offset=at), at

        def sb(name, shape, dtype=F32, at=None):
            return place(name, shape, dtype, at)[0]

        resid = sb("resid", [P, TILES, D])
        raw = sb("raw", [P, 3, WPART])
        w_hi, w_lo, w_at = [], [], []
        for b in range(2):
            t, at = place(f"w_hi{b}", [P, 3, WPART], F32R)
            w_hi.append(t)
            w_at.append(at)
            w_lo.append(sb(f"w_lo{b}", [P, 3, WPART], F32R))
        h_hi, h_at = place("h_hi", [P, JH, SLOT], F32R)
        h_lo = sb("h_lo", [P, JH, SLOT], F32R)
        xs_hi, xs_at = place("xs_hi", [P, 2, KD, SLOT], F32R)
        xs_lo, xs_lo_at = place("xs_lo", [P, 2, KD, SLOT], F32R)
        sb("z_in_rest", [P, KD, SLOT])
        x_rows, rows_at = place("x_rows", [P, 2, SLOT // BK, KD * BK])
        y_rows = sb("y_rows", [P, 2, ST, D])
        silu = sb("silu", [P, 2, 2, SLOT])
        h32 = sb("h32", [P, 2, 2, SLOT])

        z_all = sb("z_all", [P, TILES, D], at=w_at[1])
        hT_at = w_at[1] + 4 * TILES * D
        hT_hi = sb("hT_hi", [P, 2, KD, CH], F32R, at=hT_at)
        hT_lo = sb("hT_lo", [P, 2, KD, CH], F32R, at=hT_at + 8 * KD * CH)
        a_sb = sb("a_sb", [P, 2, KD, CH], at=h_at)
        y_sb = sb("y_sb", [P, 2, KD, CH], at=h_at + 8 * KD * CH)
        w_nat = sb("w_nat", [P, 3 * KD, D], at=h_at)
        wT_32 = sb("wT_32", [P, 3, KD, D], at=h_at + 8 * KD * CH)
        wT_hi = sb("wT_hi", [P, 3, KD, D], F32R, at=rows_at + 8 * ST * D)
        wT_lo = sb("wT_lo", [P, 3, KD, D], F32R, at=rows_at + 8 * ST * D + 12 * KD * D)
        z_in = [sb("z_in", [P, CH // BK, KD * BK], at=xs_lo_at + 4 * KD * SLOT)] * (NC - 2) + [
            sb("z_in_6", [P, CH // BK, KD * BK], at=hT_at + 12 * KD * CH)]
        zT = [sb("zT", [P, KD, CH], at=xs_at)] * (TILES // CT - 3) + [
            sb("zT_5", [P, KD, CH], at=hT_at + 8 * KD * CH), sb("zT_6", [P, KD, CH], at=hT_at),
            sb("zT_7", [P, KD, CH], at=hT_at + 4 * KD * CH)]
        incl = sb("incl", [P, EP, TILES], at=hT_at + 8 * KD * CH)
        cmp = sb("cmp", [P, EP, THR], at=hT_at + 8 * KD * CH + 1024)
        owner_c = sb("owner_c", [1, ROUTED, E], at=hT_at + 8 * KD * CH + 2048)
        GR = 8
        got = sb("got", [P, GR, TOP, D], at=w_at[0])

        ident = sb("ident", [P, P])
        below = sb("below", [P, P])
        ones = sb("ones", [P, P])
        zeros = sb("zeros", [P, D])
        eps = sb("eps", [P, CT])
        power = sb("power", [P, CT])
        r_nat = sb("r_nat", [E, D])
        rT = sb("rT", [P, KD, EP])
        g_nat = sb("g_nat", [KD, P])
        gT = sb("gT", [P, KD])
        warmed = sb("warmed", [P, 1])
        stats1 = sb("stats1", [P, CT, 6])
        stats2 = sb("stats2", [P, CT, 6])
        mv1 = sb("mv1", [P, TILES, 2])
        mv2 = sb("mv2", [P, TILES, 2])
        var1 = sb("var1", [P, TILES])
        scale1 = sb("scale1", [P, TILES])
        bias1 = sb("bias1", [P, TILES])
        scale2 = sb("scale2", [P, TILES])
        bias2 = sb("bias2", [P, TILES])
        p_var, p_len = (sb(n, [P, CT]) for n in ("p_var", "p_len"))
        state = sb("state", [P, KD])
        iota_i = sb("iota_i", [P, 64], I32)
        iota_f = sb("iota_f", [P, 64])
        DESC, SLOTS, THRS = iota_f[:, 0:EP], iota_f[0:1, EP:EP + ROUTED], iota_f[:, 48:48 + THR]
        assert EP + ROUTED <= 48 and THR <= 16
        logits = sb("logits", [P, TILES, EP])
        first = sb("first", [P, TOP, TILES, EP])
        tmp = sb("tmp", [P, TILES, EP])
        count = sb("count", [P, EP, TILES])
        keep = sb("keep", [P, EP, TILES])
        top = sb("top", [P, TOP, TILES])
        col = sb("col", [P, TILES])
        gap = sb("gap", [P, TILES])
        mix_w = sb("mix_w", [P, TOP, TILES])
        n_slots = sb("n_slots", [P, EP])
        s_incl = sb("s_incl", [P, EP])
        s_base = sb("s_base", [P, EP])
        pos_f = sb("pos_f", [P, TILES])
        pos = sb("pos", [P, TOP, TILES], I32)
        owner_f = sb("owner_f", [1, ROUTED])
        owner = sb("owner", [1, ROUTED], I32)
        assert base[0] <= nc.sbuf_usable_end, base[0]

        ps = ctx.enter_context(nc.psum_tensor("ps", [P, 8, 512], F32))

        def sem(name):
            return ctx.enter_context(nc.semaphore(name))

        x_in = [sem(f"x_in{g}") for g in range(NC)]
        small_in = sem("small_in")
        raw_in = [sem(f"raw_in{k}") for k in range(3)]
        consts = sem("consts")
        pool_step = sem("pool_step")
        dve_step = sem("dve_step")
        prep = sem("prep")
        prep_done = sem("prep_done")
        wT_made = sem("wT_made")
        wT_rounded = sem("wT_rounded")
        wT_split = sem("wT_split")
        mv1_taken = sem("mv1_taken")
        mv1_ready, mv2_ready = sem("mv1_ready"), sem("mv2_ready")
        scaled1 = sem("scaled1")
        h_ready1 = sem("h_ready1")
        hT_psum = sem("hT_psum")
        hT_rounded = sem("hT_rounded")
        hT_split = sem("hT_split")
        a_psum, kv_psum, q_psum = sem("a_psum"), sem("kv_psum"), sem("q_psum")
        a_ready = sem("a_ready")
        y_ready = sem("y_ready")
        o_ready = sem("o_ready")
        o_psum = sem("o_psum")
        res_ready = sem("res_ready")
        scaled2 = sem("scaled2")
        z_ready = sem("z_ready")
        z_out = [sem(f"z_out{g}") for g in range(NC)]
        z_ld = sem("z_ld")
        zT_psum = sem("zT_psum")
        zT_ready = sem("zT_ready")
        lg_psum = sem("lg_psum")
        lg_ready = sem("lg_ready")
        zeros_made = sem("zeros_made")
        zero_in = sem("zero_in")
        hot = sem("hot")
        pre_psum = sem("pre_psum")
        gap_ready = sem("gap_ready")
        mix_ready = sem("mix_ready")
        routed = sem("routed")
        scat = sem("scat")
        x_ld = [sem("x_ld0"), sem("x_ld1")]
        xT_psum = sem("xT_psum")
        xhi_ready = sem("xhi_ready")
        x_split = sem("x_split")
        whi_ready = [sem(f"whi_ready{k}") for k in range(3)]
        wlo_ready = [sem(f"wlo_ready{k}") for k in range(3)]
        gu_psum = sem("gu_psum")
        silu_ready = sem("silu_ready")
        gated = sem("gated")
        hhi_ready = sem("hhi_ready")
        h_ready = sem("h_ready")
        down_psum = sem("down_psum")
        down_free = sem("down_free")
        y_out = [sem("y_out0"), sem("y_out1")]
        got_in = [sem(f"got_in{k}") for k in range(GR)]
        mixed = sem("mixed")
        outs = sem("outs")

        PARTS = (2, 1, 0)
        PART_BANKS = (0, 1, 6)
        WARM = 18
        POOL_LO = (0, 2)
        NB0 = SA + ROUTED

        def place_of(j, p):
            return j * ST + (p % ST + p // ST * (TILES // 2))

        block = ctx.enter_context(nc.Block())

        def raw_rows(gate, up, down):
            return (gate.rearrange("(p k) h -> p k h", p=P), up.rearrange("(p k) h -> p k h", p=P),
                    down.rearrange("(j p) d -> p j d", p=P))

        raw_v = [raw[:, 0, :].rearrange("p (k h) -> p k h", k=KD),
                 raw[:, 1, :].rearrange("p (k h) -> p k h", k=KD),
                 raw[:, 2, :].rearrange("p (j d) -> p j d", j=JH)]

        @block.sync
        def _(sp):
            for g in range(NC):
                sp.dma_start(resid[:, g * CT:(g + 1) * CT, :], x_t[:, g * CT:(g + 1) * CT, :]
                             ).then_inc(x_in[g], 16)
                if g == 0:
                    sp.wait_ge(small_in, 48)

            def load_x(n, slot, dram, par):
                sp.wait_ge(xT_psum, n + 1)
                for a in range(NBK):
                    sp.dma_start(x_rows[a * BK:(a + 1) * BK, par, :, :], piece_of(dram, slot, SLOT, a)
                                 ).then_inc(x_ld[par], 16)

            for k, src in enumerate(raw_rows(sw_gate[0], sw_up[0], sw_down[0])):
                sp.dma_start(raw_v[k], src).then_inc(raw_in[k], 16)

            z_v = z_dram.rearrange("(g k p) d -> g p k d", p=P, k=CT)

            def store_z(g):
                sp.wait_ge(z_ready, g + 1)
                sp.dma_start(z_v[g], z_all[:, g * CT:(g + 1) * CT, :]).then_inc(z_out[g], 16)

            sp.wait_ge(zeros_made, 1)

            def fill(z):
                lo, hi = (ROUTED * ST * n // ZEROS for n in (z, z + 1))
                sp.dma_start(sorted_dram[lo * P:hi * P].rearrange("(k p) d -> p k d", p=P),
                             zeros[:, :].unsqueeze(1).broadcast_to([P, hi - lo, D])
                             ).then_inc(zero_in, 16)

            for z in range(ZEROS - (NC - 2)):
                fill(z)
            for g in range(NC - 1):
                store_z(g)
                sp.wait_ge(z_out[g], 16)
                if g >= 1:
                    sp.wait_ge(zT_ready, g)
                if g == NC - 2:
                    sp.wait_ge(q_psum, NC)
                for a in range(NBK):
                    sp.dma_start(z_in[g][a * BK:(a + 1) * BK, :, :], piece_of(z_dram, g, CH, a)
                                 ).then_inc(z_ld, 16)
                if g < NC - 2:
                    fill(ZEROS - (NC - 2) + g)
                if g == 0:
                    for u in range(2):
                        load_x(u, u, z_dram, u)

            def load_w(sources, m):
                for k, src in enumerate(sources):
                    sp.wait_ge(wlo_ready[k], m)
                    sp.dma_start(raw_v[k], src).then_inc(raw_in[k], 16)

            def load_expert(r, m):
                e = sp.value_load(owner[0:1, bass.ds(r, 1)], min_val=0, max_val=E - 1)
                def of(w):
                    return w[bass.ds(e, 1)].rearrange("a r c -> (a r) c")
                load_w(raw_rows(of(w_gate), of(w_up), of(w_down)), m)

            store_z(NC - 1)
            sp.wait_ge(z_out[NC - 1], 16)
            for u in range(2):
                load_x(2 + u, 2 + u, z_dram, u)
            sp.wait_ge(routed, 1)
            load_expert(0, 1)
            with sp.Fori(2, SA // 2) as i:
                for u in range(2):
                    load_x(i * 2 + u, i * 2 + u, z_dram, u)
            sp.wait_ge(scat, 16 * TOP * TILES)
            with sp.Fori(0, ROUTED // 2 - 1) as i:
                for u in range(2):
                    load_x(i * 2 + (SA + u), i * 2 + u, sorted_dram, u)
                    load_expert(i * 2 + (u + 1), i * 2 + (u + 2))
            load_x(NB0 - 2, ROUTED - 2, sorted_dram, 0)
            load_expert(ROUTED - 1, ROUTED)
            load_x(NB0 - 1, ROUTED - 1, sorted_dram, 1)
            load_w(raw_rows(sw_gate[0], sw_up[0], sw_down[0]), ROUTED + 1)
            for u in range(2):
                load_x(NB0 + u, SA + u, z_dram, u)

            def store(j):
                sp.wait_ge(mixed, j * (2 * TOP * ST) + 2 * TOP * ST)
                for half in range(2):
                    if half:
                        sp.wait_ge(down_free, j + (NB0 + 2))
                    t0 = j * ST + half * (TILES // 2)
                    sp.dma_start(out_t[:, bass.ds(t0, ST), :], resid[:, bass.ds(t0, ST), :]
                                 ).then_inc(outs, 16)

            with sp.Fori(0, SBN // 2 - 1) as i:
                for u in range(2):
                    load_x(i * 2 + (NB0 + 2 + u), i * 2 + (SA + 2 + u), z_dram, u)
                    store(i * 2 + u)
            for u in range(2):
                store(SBN - 2 + u)
            sp.wait_ge(outs, 2 * 16 * SBN)
            for u in range(2):
                sp.wait_ge(y_out[u], 16 + 16 * (ROUTED // 2))
            sp.wait_ge(zero_in, 16 * ZEROS)

        @block.gpsimd
        def _(pool):
            made = [0]

            def own(ins):
                made[0] += 1
                ins.then_inc(pool_step, 1)

            def step(ins):
                own(ins)
                pool.wait_ge(pool_step, made[0])

            own(pool.memset(ident[:, :], 0.0))
            own(pool.memset(below[:, :], 1.0))
            own(pool.memset(ones[:, :], 1.0))
            own(pool.memset(eps[:, :], EPS))
            own(pool.memset(power[:, :], -0.5))
            own(pool.iota(iota_i[:, 0:EP], pattern=[[-1, EP]], base=EP, channel_multiplier=0))
            own(pool.iota(iota_i[:, EP:48], pattern=[[1, 48 - EP]], base=0, channel_multiplier=0))
            own(pool.iota(iota_i[:, 48:64], pattern=[[SLOT, 16]], base=0, channel_multiplier=0))
            pool.wait_ge(pool_step, made[0])
            pool.affine_select(out=ident[:, :], in_=ident[:, :], compare_op=ALU.not_equal, fill=1.0,
                               base=0, pattern=[[-1, P]], channel_multiplier=1).then_inc(consts, 1)
            pool.affine_select(out=below[:, :], in_=below[:, :], compare_op=ALU.is_gt, fill=0.0,
                               base=0, pattern=[[1, P]], channel_multiplier=-1).then_inc(consts, 1)
            pool.tensor_copy(iota_f[:, :], iota_i[:, :]).then_inc(consts, 1)

            def inv_sqrt(out, a):
                step(pool.tensor_tensor(out, a, power[:, :], ALU.pow))

            def scales1(g):
                ts = slice(g * CT, (g + 1) * CT)
                pool.wait_ge(mv1_ready, g + 1)
                inv_sqrt(scale1[:, ts], var1[:, ts])
                step(pool.tensor_tensor(p_len[:, :], mv1[:, ts, 0], scale1[:, ts], ALU.mult))
                pool.tensor_scalar(bias1[:, ts], p_len[:, :], -1.0, None, ALU.mult
                                   ).then_inc(scaled1, 1)
                pool.wait_ge(scaled1, g + 1)

            def scales2(g):
                ts = slice(g * CT, (g + 1) * CT)
                pool.wait_ge(mv2_ready, g + 1)
                step(pool.tensor_tensor(p_var[:, :], mv2[:, ts, 1], eps[:, :], ALU.add))
                inv_sqrt(scale2[:, ts], p_var[:, :])
                step(pool.tensor_tensor(p_len[:, :], mv2[:, ts, 0], scale2[:, ts], ALU.mult))
                pool.tensor_scalar(bias2[:, ts], p_len[:, :], -1.0, None, ALU.mult
                                   ).then_inc(scaled2, 1)
                pool.wait_ge(scaled2, g + 1)

            def split_lo(k, m, buf):
                pool.wait_ge(whi_ready[k], m + 1)
                pool.tensor_tensor(w_lo[buf][:, k, :], raw[:, k, :], w_hi[buf][:, k, :].bitcast(F32),
                                   ALU.subtract).then_inc(wlo_ready[k], 1)

            pool.wait_ge(pool_step, made[0])
            for g in range(3):
                scales1(g)
            for g in range(NC):
                if g >= 1:
                    scales2(g - 1)
                if g + 3 < NC:
                    scales1(g + 3)
                if 4 <= g < 7:
                    split_lo(g - 4, 0, 0)
            scales2(NC - 1)
            pool.wait_ge(z_ready, NC)
            pool.wait_ge(zero_in, ZEROS * 16)
            pool.wait_ge(routed, 1)
            for t in range(TILES):
                for k in range(TOP):
                    pool.indirect_dma_start(
                        sorted_dram, bass.IndirectOffsetOnAxis(ap=pos[:, k, t:t + 1], axis=0),
                        z_all[:, t, :], None, bounds_check=ROUTED * SLOT - 1).then_inc(scat, 16)
            for k in POOL_LO:
                split_lo(k, 1, 1)
            with pool.Fori(0, ROUTED // 2) as i:
                for u in range(2):
                    for k in POOL_LO:
                        split_lo(k, i * 2 + (u + 2), u)

            for u in range(2):
                pool.wait_ge(y_out[u], 16 + 16 * (ROUTED // 2))
            for i in range(TILES // GR):
                for r in range(GR):
                    t = place_of(i * 2 + r // (2 * ST), r % (2 * ST))
                    if i:
                        j = (i - 1) * 2 + r // (2 * ST)
                        pool.wait_ge(mixed, 2 * TOP * ST * j + 2 * ST + r % (2 * ST) + 1)
                    for k in range(TOP):
                        pool.indirect_dma_start(
                            got[:, r, k, :], None, y_dram,
                            bass.IndirectOffsetOnAxis(ap=pos[:, k, t:t + 1], axis=0),
                            bounds_check=ROUTED * SLOT - 1).then_inc(got_in[r], 16)

        @block.scalar
        def _(act):
            for k, (dst, src) in enumerate((
                    (w_nat[:, :, :], w_qkva.rearrange("(e p) d -> p e d", p=P)),
                    (g_nat[:, :], gamma.rearrange("(k p) -> k p", p=P)),
                    (r_nat[:, :], router_w))):
                act.dma_start(dst, src).then_inc(small_in, 16)
            def h_rows(g):
                act.wait_ge(scaled1, g + 1)
                for t in range(g * CT, (g + 1) * CT):
                    last = act.activation(z_all[:, t, :], resid[:, t, :], ACT.Identity,
                                          scale=scale1[:, t:t + 1], bias=bias1[:, t:t + 1])
                last.then_inc(h_ready1, 1)

            act.wait_ge(consts, 3)
            act.activation(warmed[:, :], ones[:, 0:1], ACT.Sigmoid)
            h_rows(0)

            def x_hi(n, par):
                act.wait_ge(xT_psum, n + 3)
                act.activation(xs_hi[:, par, :, :], ps[:, 6, :].rearrange("p (k n) -> p k n", k=KD),
                               ACT.Copy).then_inc(xhi_ready, 1)

            def z_rows(g):
                act.wait_ge(scaled2, g + 1)
                for t in range(g * CT, (g + 1) * CT):
                    last = act.activation(z_all[:, t, :], resid[:, t, :], ACT.Identity,
                                          scale=scale2[:, t:t + 1], bias=bias2[:, t:t + 1])
                last.then_inc(z_ready, 1)

            def h_hi_part(g):
                act.wait_ge(hT_psum, g + 1)
                if g >= 2:
                    act.wait_ge(q_psum, g - 1)
                bank = 0 if g else 4
                act.activation(hT_hi[:, g % 2, :, :], ps[:, bank:bank + 2, :], ACT.Copy
                               ).then_inc(hT_rounded, 1)

            def zT_copy():
                act.wait_ge(zT_psum, 1)
                act.wait_ge(zT_ready, NC - 1)
                act.activation(zT[NC - 1][:, :, :], ps[:, 0:2, :], ACT.Copy).then_inc(zT_ready, 1)

            h_hi_part(0)
            h_rows(1)
            for g in range(NC):
                act.wait_ge(a_psum, g + 1)
                if g >= 2:
                    act.wait_ge(y_ready, g - 1)
                at = 2 + 2 * (g % 2)
                act.activation(a_sb[:, g % 2, :, :], ps[:, at:at + 2, :], ACT.Sigmoid
                               ).then_inc(a_ready, 1)
                if 1 <= g < NC - 2:
                    h_rows(g + 2)
                if g + 1 < NC:
                    h_hi_part(g + 1)
                else:
                    x_hi(0, 0)
                if g == 0:
                    h_rows(2)
                if g >= 1:
                    z_rows(g - 1)
                if 4 <= g < 7:
                    act.wait_ge(raw_in[g - 4], 16)
                    act.activation(w_hi[0][:, g - 4, :], raw[:, g - 4, :], ACT.Copy
                                   ).then_inc(whi_ready[g - 4], 1)

            def slot(n, u, r=None, m=None, load=None, last=False, between=()):
                for p in range(PAIRS):
                    q = n * PAIRS + p
                    par = p % 2
                    act.wait_ge(gu_psum, q + 1)
                    act.activation(silu[:, par, :, :], ps[:, 2 * par:2 * par + 2, 0:SLOT], ACT.Silu
                                   ).then_inc(silu_ready, 1)
                    act.wait_ge(gated, q + 3)
                    if p == 0:
                        act.wait_ge(down_psum, n + 1)
                    act.activation(h_hi[:, 2 * p:2 * p + 2, :], h32[:, par, :, :], ACT.Copy
                                   ).then_inc(hhi_ready, 1)
                    if p in between:
                        between[p]()
                if not last:
                    x_hi(n + 1, 1 - u)
                if m is not None:
                    act.wait_ge(raw_in[2], load)
                    act.activation(w_hi[u][:, 2, :], raw[:, 2, :], ACT.Copy).then_inc(whi_ready[2], 1)
                if r is not None:
                    act.wait_ge(down_psum, n + 2)
                    act.wait_ge(y_out[u], r)
                    act.activation(y_rows[:, u, :, :], ps[:, 4:6, 0:D], ACT.Copy
                                   ).then_inc(down_free, 1)
                    act.wait_ge(down_free, n + 2)
                    act.dma_start(rows_of(y_dram, n - SA), y_rows[:, u, :, :]).then_inc(y_out[u], 16)

            slot(0, 0, between={1: lambda: z_rows(NC - 1), 2: zT_copy})
            slot(1, 1)
            act.wait_ge(gap_ready, 1)
            act.activation(mix_w[:, 0, :], gap[:, :], ACT.Sigmoid).then_inc(mix_ready, 1)
            act.activation(mix_w[:, 1, :], gap[:, :], ACT.Sigmoid, scale=-1.0).then_inc(mix_ready, 1)
            with act.Fori(1, SA // 2 - 1) as i:
                for u in range(2):
                    slot(i * 2 + u, u)
            slot(SA - 2, 0)
            act.wait_ge(scat, 16 * TOP * TILES)
            slot(SA - 1, 1, m=1, load=32)
            with act.Fori(0, ROUTED // 2) as i:
                for u in range(2):
                    slot(i * 2 + (SA + u), u, r=i * 16 + 16, m=i * 2 + (2 + u),
                         load=i * 32 + (48 + 16 * u))
            with act.Fori(0, SBN // 2 - 1) as i:
                for u in range(2):
                    slot(i * 2 + (NB0 + u), u)
            slot(NB0 + SBN - 2, 0)
            slot(NB0 + SBN - 1, 1, last=True)

        @block.tensor
        def _(pe):
            pe.wait_ge(consts, 3)
            pe.wait_ge(small_in, 48)
            pe.transpose(ps[:, 7, 0:KD], g_nat[:, :], ident[0:KD, 0:KD])
            for k in range(KD):
                last = pe.transpose(ps[:, 7, KD + k * E:KD + k * E + E],
                                    r_nat[:, :].rearrange("e (p k) -> e k p", k=KD)[:, k],
                                    ident[0:E, 0:E])
            last.then_inc(prep, 1)
            for part, bank in zip(PARTS, PART_BANKS):
                for k in range(KD):
                    for e in range(KD):
                        last = pe.transpose(ps[:, bank, k * D + e * P:k * D + (e + 1) * P],
                                            w_nat[:, part * KD + e, k * P:(k + 1) * P], ident[:, :])
                last.then_inc(prep, 1)

            def turn_h(g):
                pe.wait_ge(h_ready1, g + 1)
                if g >= 1:
                    pe.wait_ge(hT_split, g)
                if g >= 4:
                    pe.wait_ge(lg_ready, g - 3)
                bank = 0 if g else 4
                for kd in range(KD):
                    for k in range(CT):
                        last = pe.transpose(ps[:, bank + kd, k * P:(k + 1) * P],
                                            z_all[:, g * CT + k, kd * P:(kd + 1) * P], ident[:, :])
                last.then_inc(hT_psum, 1)

            def turn_last_z():
                pe.wait_ge(z_ready, NC)
                pe.wait_ge(gated, 5)
                for kd in range(KD):
                    for k in range(CT):
                        z = z_all[:, (NC - 1) * CT + k, :].rearrange("p (i k) -> p k i", k=KD)
                        last = pe.transpose(ps[:, kd, k * P:(k + 1) * P], z[:, kd], ident[:, :])
                last.then_inc(zT_psum, 1)

            def route(g, bank):
                pe.wait_ge(zT_ready, g + 1)
                if g >= 1:
                    pe.wait_ge(lg_ready, g)
                for k in range(CT):
                    for kd in range(KD):
                        last = pe.matmul(ps[:, bank, k * EP:k * EP + E],
                                         zT[g][:, kd, k * P:(k + 1) * P], rT[:, kd, 0:E],
                                         start=kd == 0, stop=kd == KD - 1)
                last.then_inc(lg_psum, 1)

            def project(g, part, bank, signal):
                c = g % 2
                for e in range(KD):
                    at = e * P
                    terms = [(w, h, kd) for kd in range(KD)
                             for w, h in ((wT_hi, hT_hi), (wT_hi, hT_lo), (wT_lo, hT_hi))]
                    for i, (w, h, kd) in enumerate(terms):
                        last = pe.matmul(ps[:, bank + e, :], w[:, part, kd, at:at + P], h[:, c, kd, :],
                                         start=i == 0, stop=i == len(terms) - 1)
                last.then_inc(signal, 1)

            def turn_back(g, bank):
                pe.wait_ge(o_ready, g + 1)
                if g >= 1:
                    pe.wait_ge(res_ready, g)
                for k in range(CT):
                    for e in range(KD):
                        at = (k % 2) * D + e * P
                        last = pe.transpose(ps[:, bank + k // 2, at:at + P],
                                            y_sb[:, g % 2, e, k * P:(k + 1) * P], ident[:, :])
                last.then_inc(o_psum, 1)

            turn_h(0)
            for _ in range(WARM):
                pe.transpose(ps[:, 3, 0:P], ident[:, :], ident[:, :])
            for g in range(NC):
                one = 2 + 2 * (g % 2)
                two = 6 - one
                pe.wait_ge(hT_split, g + 1)
                if g >= 1:
                    pe.wait_ge(y_ready, g)
                if g == 0:
                    pe.wait_ge(wT_split, 1)
                project(g, 2, one, a_psum)
                if g >= 1:
                    turn_back(g - 1, 6)
                if g >= 3:
                    route(g - 3, 0)
                if g >= 1:
                    pe.wait_ge(o_ready, g)
                if g == 0:
                    pe.wait_ge(wT_split, 2)
                project(g, 1, two, kv_psum)
                if g + 1 < NC:
                    turn_h(g + 1)
                pe.wait_ge(a_ready, g + 1)
                if g == 0:
                    pe.wait_ge(wT_split, 3)
                project(g, 0, one, q_psum)

            def last_back():
                turn_back(NC - 1, 4)

            def last_routes(g):
                pe.wait_ge(res_ready, NC - 1)
                route(g, 7)

            def ranks():
                pe.wait_ge(hot, 1)
                flat = tmp[:, :, :].rearrange("p t e -> p (t e)")
                pe.matmul(ps[:, 7, 0:TILES * EP], below[:, :], flat, start=True, stop=True)
                pe.matmul(ps[:, 7, TILES * EP:2 * TILES * EP], ones[:, :], flat, start=True, stop=True
                          ).then_inc(pre_psum, 1)

            def slot(n, u, buf, m=None, between=(), down=None):
                pe.wait_ge(x_split, n + 1)
                if m is not None:
                    for k in range(2):
                        pe.wait_ge(wlo_ready[k], m + 1)
                hi, lo = w_hi[buf], w_lo[buf]
                for p in range(PAIRS):
                    q = n * PAIRS + p
                    pe.wait_ge(gated, q + 1)
                    for j in (2 * p, 2 * p + 1):
                        if j - 1 in between:
                            between[j - 1]()
                        for part in range(2):
                            o = ps[:, 2 * (p % 2) + j % 2, part * SLOT:(part + 1) * SLOT]
                            at = [kd * H + j * P for kd in range(KD)]
                            terms = [(w, xx, kd) for kd in range(KD)
                                     for w, xx in ((hi, xs_hi), (hi, xs_lo), (lo, xs_hi))]
                            for i, (w, xx, kd) in enumerate(terms):
                                last = pe.matmul(o, w[:, part, at[kd]:at[kd] + P], xx[:, u, kd, :],
                                                 start=i == 0, stop=i == len(terms) - 1)
                    last.then_inc(gu_psum, 1)
                if JH - 1 in between:
                    between[JH - 1]()
                if m is not None:
                    pe.wait_ge(wlo_ready[2], m + 1)
                if down is None:
                    pe.wait_ge(down_free, n + 1)
                else:
                    pe.wait_ge(res_ready, NC)
                for p in range(PAIRS):
                    pe.wait_ge(h_ready, n * PAIRS + (p + 3))
                    for j in (2 * p, 2 * p + 1):
                        for t in range(ST):
                            terms = ((h_hi, hi), (h_hi, lo), (h_lo, hi))
                            for i, (hh, w) in enumerate(terms):
                                last = pe.matmul(ps[:, 4 + t, 0:D], hh[:, j, t * P:(t + 1) * P],
                                                 w[:, 2, j * D:(j + 1) * D],
                                                 start=j == 0 and i == 0,
                                                 stop=j == JH - 1 and i == len(terms) - 1)
                    if p == 0 and down is not None:
                        down()
                last.then_inc(down_psum, 1)

            for k in range(3):
                pe.wait_ge(wlo_ready[k], 1)
            slot(0, 0, 0, between={0: last_back, 2: lambda: last_routes(NC - 3),
                                   6: lambda: last_routes(NC - 2), JH - 1: turn_last_z},
                 down=lambda: last_routes(NC - 1))
            slot(1, 1, 0, between={1: ranks})
            with pe.Fori(1, SA // 2) as i:
                for u in range(2):
                    slot(i * 2 + u, u, 0)
            with pe.Fori(0, ROUTED // 2) as i:
                slot(i * 2 + SA, 0, 1, m=i * 2 + 1)
                slot(i * 2 + (SA + 1), 1, 0, m=i * 2 + 2)
            slot(NB0, 0, 1, m=ROUTED + 1)
            slot(NB0 + 1, 1, 1)
            with pe.Fori(1, SBN // 2) as i:
                for u in range(2):
                    slot(i * 2 + (NB0 + u), u, 1)

        @block.vector
        def _(dve):
            for s, n in ((xT_psum, 2), (gated, 2), (h_ready, 2), (down_psum, 1), (down_free, 1),
                         (y_out[0], 16), (y_out[1], 16)):
                dve.sem_inc(s, n)
            made = [0]

            def step(ins):
                made[0] += 1
                ins.then_inc(dve_step, 1)
                dve.wait_ge(dve_step, made[0])

            dve.memset(zeros[:, :], 0.0).then_inc(zeros_made, 1)
            dve.memset(logits[:, :, E:EP], LOWEST)
            dve.memset(keep[:, :, 1:TILES], 1.0)
            step(dve.memset(keep[:, :, 0:1], 0.0))

            def statistics(g, stats, mv, signal):
                if g >= 1:
                    dve.wait_ge(signal, g)
                for k in range(CT):
                    last = dve.bn_stats(stats[:, k, :], resid[:, g * CT + k, :])
                step(last)
                for k in range(CT):
                    last = dve.bn_aggr(mv[:, g * CT + k, :], stats[:, k, :])
                last.then_inc(signal, 1)
                dve.wait_ge(signal, g + 1)

            def statistics1(g):
                dve.wait_ge(x_in[g], 16)
                statistics(g, stats1, mv1, mv1_taken)
                ts = slice(g * CT, (g + 1) * CT)
                step(dve.tensor_scalar(var1[:, ts], mv1[:, ts, 1], EPS, TINY2 / D, ALU.add, ALU.mult))
                dve.tensor_tensor(var1[:, ts], var1[:, ts], mv1[:, ts, 1], ALU.max
                                  ).then_inc(mv1_ready, 1)

            def h_lo_part(g):
                dve.wait_ge(hT_rounded, g + 1)
                bank = 0 if g else 4
                dve.tensor_tensor(hT_lo[:, g % 2, :, :], ps[:, bank:bank + 2, :],
                                  hT_hi[:, g % 2, :, :].bitcast(F32), ALU.subtract
                                  ).then_inc(hT_split, 1)

            def residual(g, bank=6, stats=True):
                dve.wait_ge(o_psum, g + 1)
                rows = resid[:, g * CT:(g + 1) * CT, :]
                back = ps[:, bank:bank + 2, :].rearrange("p b (k d) -> p (b k) d", d=D)
                dve.tensor_tensor(rows, back, rows, ALU.add).then_inc(res_ready, 1)
                if stats:
                    statistics2(g)

            def statistics2(g):
                dve.wait_ge(res_ready, g + 1)
                statistics(g, stats2, mv2, mv2_ready)

            def turn_z(g):
                dve.wait_ge(z_ld, LD * (g + 1))
                if g >= 1:
                    dve.wait_ge(lg_psum, g)
                for k in range(KD):
                    last = dve.transpose(zT[g][:, k, :].rearrange("p (b j) -> p b j", j=BK),
                                         z_in[g][:, :, :].rearrange("p b (i k) -> p k b i", k=KD)[:, k])
                last.then_inc(zT_ready, 1)

            def take_logits(g, bank):
                dve.wait_ge(lg_psum, g + 1)
                dve.tensor_copy(logits[:, g * CT:(g + 1) * CT, 0:E],
                                ps[:, bank, 0:CT * EP].rearrange("p (k e) -> p k e", e=EP)[:, :, 0:E]
                                ).then_inc(lg_ready, 1)

            def scan(g):
                c, kv = g % 2, 4 - 2 * (g % 2)
                dve.wait_ge(a_ready, g + 1)
                dve.wait_ge(kv_psum, g + 1)
                if g >= 2:
                    dve.wait_ge(o_psum, g - 1)
                for e in range(KD):
                    last = dve.tensor_tensor_scan(y_sb[:, c, e, :], a_sb[:, c, e, :], ps[:, kv + e, :],
                                                  state[:, e:e + 1] if c else 0.0, ALU.mult, ALU.add)
                last.then_inc(y_ready, 1)
                dve.wait_ge(y_ready, g + 1)
                if c == 0:
                    step(dve.tensor_copy(state[:, :], y_sb[:, c, :, CH - 1]))

            def times_q(g):
                c, q = g % 2, 2 + 2 * (g % 2)
                dve.wait_ge(q_psum, g + 1)
                dve.tensor_tensor(y_sb[:, c, :, :], ps[:, q:q + 2, :], y_sb[:, c, :, :], ALU.mult
                                  ).then_inc(o_ready, 1)

            def turn_x(par, nth):
                dve.wait_ge(x_ld[par], nth)
                for k in range(KD):
                    half = ps[:, 6, k * SLOT:(k + 1) * SLOT]
                    last = dve.transpose(half.rearrange("p (b j) -> p b j", j=BK),
                                         x_rows[:, par, :, :].rearrange("p b (i k) -> p k b i", k=KD)[:, k])
                last.then_inc(xT_psum, 1)

            def x_lo(n, par):
                dve.wait_ge(xhi_ready, n + 1)
                dve.tensor_tensor(xs_lo[:, par, :, :], ps[:, 6, :].rearrange("p (k n) -> p k n", k=KD),
                                  xs_hi[:, par, :, :].bitcast(F32), ALU.subtract).then_inc(x_split, 1)

            def prepare(nth, part):
                dve.wait_ge(prep, nth + 2)
                turned = ps[:, PART_BANKS[nth], :].rearrange("p (k n) -> p k n", k=KD)
                dve.tensor_tensor(wT_32[:, part, :, :], turned,
                                  gT[:, :].unsqueeze(2).broadcast_to([P, KD, D]), ALU.mult
                                  ).then_inc(wT_made, 1)
                dve.wait_ge(wT_made, nth + 1)
                dve.tensor_copy(wT_hi[:, part, :, :], wT_32[:, part, :, :]).then_inc(wT_rounded, 1)
                dve.wait_ge(wT_rounded, nth + 1)
                dve.tensor_tensor(wT_lo[:, part, :, :], wT_32[:, part, :, :],
                                  wT_hi[:, part, :, :].bitcast(F32), ALU.subtract).then_inc(wT_split, 1)

            statistics1(0)
            dve.wait_ge(prep, 1)
            dve.tensor_copy(gT[:, :], ps[:, 7, 0:KD])
            dve.tensor_copy(rT[:, :, 0:E], ps[:, 7, KD:KD + KD * E].rearrange("p (k e) -> p k e", k=KD)
                            ).then_inc(prep_done, 1)
            dve.wait_ge(prep_done, 1)
            prepare(0, PARTS[0])
            prepare(1, PARTS[1])
            h_lo_part(0)
            statistics1(1)
            prepare(2, PARTS[2])
            statistics1(2)
            for g in range(NC):
                if g >= 1:
                    residual(g - 1)
                if g >= 3:
                    take_logits(g - 3, 0)
                if g == NC - 1:
                    turn_x(0, LD)
                scan(g)
                if g + 1 < NC:
                    h_lo_part(g + 1)
                else:
                    x_lo(0, 0)
                times_q(g)
                if g >= 2:
                    turn_z(g - 2)
                if g + 3 < NC:
                    statistics1(g + 3)
            residual(NC - 1, 4, stats=False)

            def over_experts(a):
                return a.unsqueeze(2).broadcast_to([P, TILES, EP])

            desc = DESC.unsqueeze(1).broadcast_to([P, TILES, EP])

            def choose(k):
                if k == 0:
                    dve.wait_ge(lg_ready, NC)
                    dve.wait_ge(consts, 3)
                step(dve.tensor_reduce(top[:, k, :], logits[:, :, :], AX_X, ALU.max))
                step(dve.tensor_tensor(tmp[:, :, :], logits[:, :, :], over_experts(top[:, k, :]),
                                       ALU.is_equal))
                step(dve.tensor_tensor(tmp[:, :, :], tmp[:, :, :], desc, ALU.mult))
                step(dve.tensor_reduce(col[:, :], tmp[:, :, :], AX_X, ALU.max))
                step(dve.tensor_tensor(first[:, k, :, :], over_experts(col[:, :]), desc, ALU.is_equal))
                if k == 0:
                    step(dve.scalar_tensor_tensor(out=logits[:, :, :], in0=first[:, 0, :, :],
                                                  scalar=LOWEST, in1=logits[:, :, :],
                                                  op0=ALU.mult, op1=ALU.add))
                else:
                    dve.tensor_tensor(gap[:, :], top[:, 0, :], top[:, 1, :], ALU.subtract
                                      ).then_inc(gap_ready, 1)
                    dve.tensor_tensor(tmp[:, :, :], first[:, 0, :, :], first[:, 1, :, :], ALU.add
                                      ).then_inc(hot, 1)

            def rank():
                dve.wait_ge(pre_psum, 1)
                total = ps[:, 7, TILES * EP:2 * TILES * EP].rearrange("p (t e) -> p e t", e=EP)
                step(dve.tensor_copy(count[:, :, :], total))
                step(dve.tensor_tensor_scan(incl[:, :, :].rearrange("p e t -> p (e t)"),
                                            keep[:, :, :].rearrange("p e t -> p (e t)"),
                                            count[:, :, :].rearrange("p e t -> p (e t)"),
                                            0.0, ALU.mult, ALU.add))
                step(dve.tensor_tensor(cmp[:, :, :], incl[:, :, TILES - 1:TILES].broadcast_to([P, EP, THR]),
                                       THRS.unsqueeze(1).broadcast_to([P, EP, THR]), ALU.is_gt))
                step(dve.tensor_reduce(n_slots[:, :], cmp[:, :, :], AX_X, ALU.add))
                step(dve.tensor_tensor_scan(s_incl[:, :], ones[:, 0:EP], n_slots[:, :], 0.0,
                                            ALU.mult, ALU.add))
                step(dve.tensor_tensor(s_base[:, :], s_incl[:, :], n_slots[:, :], ALU.subtract))
                step(dve.tensor_scalar(s_base[:, :], s_base[:, :], float(SLOT), None, ALU.mult))

            def places():
                before = ps[:, 7, 0:TILES * EP].rearrange("p (t e) -> p t e", e=EP)
                step(dve.tensor_tensor(count[:, :, :], incl[:, :, :], count[:, :, :], ALU.subtract))
                step(dve.tensor_tensor(count[:, :, :], count[:, :, :],
                                       s_base[:, :].unsqueeze(2).broadcast_to([P, EP, TILES]), ALU.add))
                step(dve.tensor_tensor(tmp[:, :, :], before, count[:, :, :].rearrange("p e t -> p t e"),
                                       ALU.add))
                for k in range(TOP):
                    step(dve.tensor_tensor(first[:, k, :, :], first[:, k, :, :], tmp[:, :, :], ALU.mult))
                    step(dve.tensor_reduce(pos_f[:, :], first[:, k, :, :], AX_X, ALU.add))
                    step(dve.tensor_copy(pos[:, k, :], pos_f[:, :]))
                step(dve.tensor_tensor(owner_c[:, :, :],
                                       s_incl[0:1, 0:E].unsqueeze(1).broadcast_to([1, ROUTED, E]),
                                       SLOTS.unsqueeze(2).broadcast_to([1, ROUTED, E]), ALU.is_le))
                step(dve.tensor_reduce(owner_f[:, :], owner_c[:, :, :], AX_X, ALU.add))
                step(dve.tensor_scalar(owner_f[:, :], owner_f[:, :], float(E - 1), None, ALU.min))
                dve.tensor_copy(owner[:, :], owner_f[:, :]).then_inc(routed, 1)

            def mix(j, u, nth):
                for k in range(TOP):
                    for p in range(2 * ST):
                        r = u * 2 * ST + p
                        if k == 0:
                            dve.wait_ge(got_in[r], nth)
                        else:
                            dve.wait_ge(mixed, j * (2 * TOP * ST) + (p + 1))
                        t = place_of(j, p)
                        row = resid[:, bass.ds(t, 1), :]
                        dve.scalar_tensor_tensor(out=row, in0=got[:, r, k:k + 1, :],
                                                 scalar=mix_w[:, k, bass.ds(t, 1)], in1=row,
                                                 op0=ALU.mult, op1=ALU.add).then_inc(mixed, 1)

            def split_hi(k, buf, load):
                dve.wait_ge(raw_in[k], load)
                dve.tensor_copy(w_hi[buf][:, k, :], raw[:, k, :]).then_inc(whi_ready[k], 1)

            def split_lo(k, m, buf, half):
                cols = slice(half * WPART // 2, (half + 1) * WPART // 2)
                dve.wait_ge(whi_ready[k], m + 1)
                ins = dve.tensor_tensor(w_lo[buf][:, k, cols], raw[:, k, cols],
                                        w_hi[buf][:, k, cols].bitcast(F32), ALU.subtract)
                if half:
                    ins.then_inc(wlo_ready[k], 1)

            def slot(n, u, nth, m=None, load=None, shared=None, back=None, between=()):
                for p in range(PAIRS):
                    q = n * PAIRS + p
                    par = p % 2
                    dve.wait_ge(silu_ready, q + 1)
                    dve.wait_ge(h_ready, q + 1)
                    dve.tensor_tensor(h32[:, par, :, :], ps[:, 2 * par:2 * par + 2, SLOT:2 * SLOT],
                                      silu[:, par, :, :], ALU.mult).then_inc(gated, 1)
                    if ("gated", p) in between:
                        between["gated", p]()
                    if m is not None and p < 2:
                        dve.wait_ge(gu_psum, n * PAIRS)
                        split_hi(p, u, load)
                    if m is not None and p >= 2:
                        split_lo(1, m, u, p - 2)
                    dve.wait_ge(hhi_ready, q + 1)
                    dve.tensor_tensor(h_lo[:, 2 * p:2 * p + 2, :], h32[:, par, :, :],
                                      h_hi[:, 2 * p:2 * p + 2, :].bitcast(F32), ALU.subtract
                                      ).then_inc(h_ready, 1)
                    if p in between:
                        between[p]()
                    if p == PAIRS - 2 and nth is not None:
                        dve.wait_ge(x_split, n + 1)
                        turn_x(1 - u, nth)
                if nth is not None:
                    x_lo(n + 1, 1 - u)
                if "down" in between:
                    between["down"]()
                if back is not None:
                    mix(back * 2 + u, u, back * (16 * TOP) + 16 * TOP)
                if shared is not None:
                    dve.wait_ge(down_psum, n + 2)
                    if back is not None:
                        dve.wait_ge(mixed, back * (4 * TOP * ST) + 2 * TOP * ST * (u + 1))
                    rows = resid[:, bass.ds(shared, ST), :]
                    dve.tensor_tensor(rows, ps[:, 4:6, 0:D], rows, ALU.add).then_inc(down_free, 1)
                    dve.wait_ge(down_free, n + 2)

            def choices():
                take_logits(NC - 1, 7)
                for k in range(TOP):
                    choose(k)

            def logits_and_z():
                take_logits(NC - 3, 7)
                turn_z(NC - 2)

            slot(0, 0, LD, shared=0, between={
                ("gated", 0): lambda: statistics2(NC - 1), 1: logits_and_z,
                2: lambda: take_logits(NC - 2, 7), "down": choices})
            slot(1, 1, 2 * LD, shared=ST, between={0: rank, "down": places})
            with dve.Fori(1, SA // 2 - 1) as i:
                for u in range(2):
                    slot(i * 2 + u, u, i * LD + LD * (1 + u), shared=i * (2 * ST) + u * ST)
            R0 = SA // 2
            slot(SA - 2, 0, R0 * LD, shared=(SA - 2) * ST)
            dve.wait_ge(scat, 16 * TOP * TILES)
            slot(SA - 1, 1, (R0 + 1) * LD, m=1, load=32, shared=(SA - 1) * ST)
            with dve.Fori(0, ROUTED // 2) as i:
                for u in range(2):
                    slot(i * 2 + (SA + u), u, i * LD + LD * (R0 + 1 + u), m=i * 2 + (2 + u),
                         load=i * 32 + (48 + 16 * u))
            B0 = NB0 // 2
            dve.wait_ge(mix_ready, TOP)
            with dve.Fori(0, SBN // 2 - 1) as i:
                for u in range(2):
                    slot(i * 2 + (NB0 + u), u, i * LD + LD * (B0 + 1 + u),
                         shared=i * (2 * ST) + (TILES // 2 + u * ST), back=i)
            i = SBN // 2 - 1
            for u in range(2):
                slot(i * 2 + NB0 + u, u, None if u else LD * (B0 + 1 + i),
                     shared=i * 2 * ST + TILES // 2 + u * ST, back=i)


_INS = ['L0_attn_x', 'L0_attn_w_qkva', 'L0_attn_gamma', 'L0_ffn_router_w', 'L0_ffn_w_gate',
        'L0_ffn_w_up', 'L0_ffn_w_down', 'L0_ffn_sw_gate', 'L0_ffn_sw_up', 'L0_ffn_sw_down']


def kernel(**inputs):
    import numpy as _np
    import concourse.bacc as _bacc
    from concourse import mybir as _mybir
    from concourse.bass_utils import run_bass_kernel_spmd as _run

    nc = _bacc.Bacc("TRN2", target_bir_lowering=False, num_devices=1)
    arrays, args = {}, []
    for name in _INS:
        a = _np.ascontiguousarray(inputs[name])
        arrays[f"in_{name}_dram"] = a
        args.append(nc.dram_tensor(f"in_{name}_dram", a.shape, _mybir.dt.from_np(a.dtype), kind="ExternalInput").ap())
    shape = inputs['L0_attn_x'].shape
    args.append(nc.dram_tensor("out_0_dram", shape, _mybir.dt.float32, kind="ExternalOutput").ap())
    preln_scan_moe_kernel(nc, *args)
    r = _run(nc, [arrays], core_ids=[0])
    return r.results[0]["out_0_dram"]
```
